# Optimizing a Trainium2 kernel written in Bass

```python
import numpy as np
import jax
import jax.numpy as jnp

def _softmax(x, axis=-1):
    return jax.nn.softmax(x, axis=axis)

def _gelu(x):
    return jax.nn.gelu(x, approximate=True)

def _silu(x):
    return jax.nn.silu(x)

def _sigmoid(x):
    return jax.nn.sigmoid(x)

def _layernorm(x, axis=-1, eps=1e-05):
    m = jnp.mean(x, axis=axis, keepdims=True)
    v = jnp.var(x, axis=axis, keepdims=True)
    return (x - m) / jnp.sqrt(v + eps)

def _scatter_add(tgt, idx, src, axis=0):
    return tgt.at[idx].add(src)

def _segment_sum(src, seg, n):
    return jax.ops.segment_sum(src, seg, n)
kernel_name = 'mk_decoder_preln_d1_seqx_r8_86183f'

def setup_inputs(seed: int=0):
    np.random.seed(seed)
    _w = jnp.asarray

    def _rec_inputs():
        import jax
        import jax.numpy as jnp
        _rk = jax.random.key(seed)
        x = 7.22e-05 + 1 * jax.random.normal(jax.random.fold_in(_rk, 1), (8, 128, 512), jnp.float32)
        _lenS = 128 - jax.random.randint(jax.random.fold_in(_rk, 7), (8,), 0, max(1, 128 // 4) + 1, jnp.int32)
        _lenS2 = 128 - jax.random.randint(jax.random.fold_in(_rk, 8), (8,), 0, max(1, 128 // 4) + 1, jnp.int32)
        _ctx_4096P = jax.random.normal(jax.random.fold_in(_rk, 11), (8, 16, 512), jnp.float32)
        _ctx_4096c = jax.random.dirichlet(jax.random.fold_in(_rk, 511), 0.3 * jnp.ones((16,), jnp.float32), (8, 128))
        _ctx_4096t = jnp.einsum('bsk,bkd->bsd', _ctx_4096c, _ctx_4096P)
        _ctx_4096t = _ctx_4096t * jax.lax.rsqrt(jnp.mean(jnp.square(_ctx_4096t)) + 1e-12) * 0.953939
        ctx_4096 = 4.13588e-05 + 0.999923 * (_ctx_4096t + 0.3 * jax.random.normal(jax.random.fold_in(_rk, 611), (8, 128, 512), jnp.float32))
        _validS = jnp.arange(128)[None, :] < _lenS[:, None]
        _validS2 = jnp.arange(128)[None, :] < _lenS2[:, None]
        _causal = jnp.tril(jnp.ones((128, 128), dtype=bool))
        mask_BxSxS2_bk0 = jnp.logical_not(jnp.broadcast_to(_validS2[:, None, :], (8, 128, 128)))
        return (x, ctx_4096, mask_BxSxS2_bk0)
    x, ctx_4096, mask_BxSxS2_bk0 = _rec_inputs()

    def _L0_attn_setup():
        import jax, jax.numpy as jnp
        import numpy as np
        from jax import lax
        BLOCK_LEN = 128
        NEG_INF = -1000000000.0
        key = jax.random.key(seed)
        ks = jax.random.split(key, 8)
        N, L, Dm = (2, 1024, 512)
        W, H, dh = (128, 16, 64)
        s = lambda fan: 1.0 / np.sqrt(fan)
        return {'inputs': jax.random.normal(ks[0], (N, L, Dm), jnp.float32), 'conv_w': jax.random.normal(ks[1], (3, Dm, 3 * W), jnp.float32) * s(3 * Dm), 'conv_b': jnp.zeros((3 * W,), jnp.float32), 'wq': jax.random.normal(ks[2], (W, H, dh), jnp.float32) * s(W), 'bq': jnp.zeros((H, dh), jnp.float32), 'wk': jax.random.normal(ks[3], (W, H, dh), jnp.float32) * s(W), 'bk': jnp.zeros((H, dh), jnp.float32), 'wv': jax.random.normal(ks[4], (W, H, dh), jnp.float32) * s(W), 'bv': jnp.zeros((H, dh), jnp.float32), 'wo': jax.random.normal(ks[5], (H, dh, W), jnp.float32) * s(H * dh), 'bo': jnp.zeros((W,), jnp.float32), 'proj_w': jax.random.normal(ks[6], (W, Dm), jnp.float32) * s(W), 'proj_b': jnp.zeros((Dm,), jnp.float32)}
    _L0_attn_all = _L0_attn_setup()
    _L0_attn_in = {k: v for k, v in _L0_attn_all.items() if k in ('conv_w', 'conv_b', 'wq', 'bq', 'wk', 'bk', 'wv', 'bv', 'wo', 'bo', 'proj_w', 'proj_b')}
    del _L0_attn_all

    def _L0_xattn_setup():
        import jax, jax.numpy as jnp
        import numpy as np
        B, LQ, LK, D, H, DH = (2, 128, 128, 512, 32, 128)
        EPS = 1e-05

        def _rmsnorm(x, weight):
            var = jnp.mean(jnp.square(x), axis=-1, keepdims=True)
            return x * jax.lax.rsqrt(var + EPS) * weight
        key = jax.random.key(seed)
        ks = jax.random.split(key, 8)
        scale = 0.02
        return {'hidden_states': jax.random.normal(ks[0], (B, LQ, D), jnp.float32), 'key_value_states': jax.random.normal(ks[1], (B, LK, D), jnp.float32), 'attention_mask': jax.random.randint(ks[2], (B, LQ, LK), 0, 2) > 0, 'position_bias': jax.random.normal(ks[3], (H, LQ, LK), jnp.float32), 'ln_weight': jnp.ones((D,), jnp.float32), 'w_q': jax.random.normal(ks[4], (H * DH, D), jnp.float32) * scale, 'w_k': jax.random.normal(ks[5], (H * DH, D), jnp.float32) * scale, 'w_v': jax.random.normal(ks[6], (H * DH, D), jnp.float32) * scale, 'w_out': jax.random.normal(ks[7], (D, H * DH), jnp.float32) * scale}
    _L0_xattn_all = _L0_xattn_setup()
    _L0_xattn_in = {k: v for k, v in _L0_xattn_all.items() if k in ('position_bias', 'ln_weight', 'w_q', 'w_k', 'w_v', 'w_out')}
    del _L0_xattn_all

    def _L0_ffn_setup():
        import jax, jax.numpy as jnp
        import numpy as np
        ALPHA = 32
        R = 16
        SCALING = ALPHA / R
        key = jax.random.key(seed)
        k1, k2, k3, k4 = jax.random.split(key, 4)
        B_, S, D = (4, 256, 512)
        H, r, O = (8, R, 512)
        x = jax.random.normal(k1, (B_, S, D), dtype=jnp.float32)
        A = jax.random.normal(k2, (H, r, D), dtype=jnp.float32) * 0.02
        Bm = jax.random.normal(k3, (H, O, r), dtype=jnp.float32) * 0.02
        Wr = jax.random.normal(k4, (H, D), dtype=jnp.float32) * 0.02
        br = jnp.zeros((H,), dtype=jnp.float32)
        return {'x': x, 'A': A, 'B': Bm, 'Wr': Wr, 'br': br}
    _L0_ffn_all = _L0_ffn_setup()
    _L0_ffn_in = {k: v for k, v in _L0_ffn_all.items() if k in ('A', 'B', 'Wr', 'br')}
    del _L0_ffn_all
    return {'x': x, 'ctx_4096': ctx_4096, 'mask_BxSxS2_bk0': mask_BxSxS2_bk0, 'L0_attn_conv_w': _L0_attn_in['conv_w'], 'L0_attn_conv_b': _L0_attn_in['conv_b'], 'L0_attn_wq': _L0_attn_in['wq'], 'L0_attn_bq': _L0_attn_in['bq'], 'L0_attn_wk': _L0_attn_in['wk'], 'L0_attn_bk': _L0_attn_in['bk'], 'L0_attn_wv': _L0_attn_in['wv'], 'L0_attn_bv': _L0_attn_in['bv'], 'L0_attn_wo': _L0_attn_in['wo'], 'L0_attn_bo': _L0_attn_in['bo'], 'L0_attn_proj_w': _L0_attn_in['proj_w'], 'L0_attn_proj_b': _L0_attn_in['proj_b'], 'L0_xattn_position_bias': _L0_xattn_in['position_bias'], 'L0_xattn_ln_weight': _L0_xattn_in['ln_weight'], 'L0_xattn_w_q': _L0_xattn_in['w_q'], 'L0_xattn_w_k': _L0_xattn_in['w_k'], 'L0_xattn_w_v': _L0_xattn_in['w_v'], 'L0_xattn_w_out': _L0_xattn_in['w_out'], 'L0_ffn_A': _L0_ffn_in['A'], 'L0_ffn_B': _L0_ffn_in['B'], 'L0_ffn_Wr': _L0_ffn_in['Wr'], 'L0_ffn_br': _L0_ffn_in['br']}

def reference(x, ctx_4096, mask_BxSxS2_bk0, L0_attn_conv_w, L0_attn_conv_b, L0_attn_wq, L0_attn_bq, L0_attn_wk, L0_attn_bk, L0_attn_wv, L0_attn_bv, L0_attn_wo, L0_attn_bo, L0_attn_proj_w, L0_attn_proj_b, L0_xattn_position_bias, L0_xattn_ln_weight, L0_xattn_w_q, L0_xattn_w_k, L0_xattn_w_v, L0_xattn_w_out, L0_ffn_A, L0_ffn_B, L0_ffn_Wr, L0_ffn_br):
    import jax
    import jax.numpy as jnp

    def _L0_attn_ref(inputs, conv_w, conv_b, wq, bq, wk, bk, wv, bv, wo, bo, proj_w, proj_b):
        import jax, jax.numpy as jnp
        import numpy as np
        from jax import lax
        BLOCK_LEN = 128
        NEG_INF = -1000000000.0
        N, L, Dm = inputs.shape
        x = lax.conv_general_dilated(inputs, conv_w, window_strides=(1,), padding='SAME', dimension_numbers=('NWC', 'WIO', 'NWC')) + conv_b
        q, k, v = jnp.split(x, 3, axis=-1)
        W_ = q.shape[-1]
        nb = L // BLOCK_LEN
        q = q.reshape(N * nb, BLOCK_LEN, W_)
        k = k.reshape(N * nb, BLOCK_LEN, W_)
        v = v.reshape(N * nb, BLOCK_LEN, W_)
        dh = wq.shape[-1]
        qh = jnp.einsum('btd,dhe->bthe', q, wq) + bq
        kh = jnp.einsum('btd,dhe->bthe', k, wk) + bk
        vh = jnp.einsum('btd,dhe->bthe', v, wv) + bv
        scale = 1.0 / jnp.sqrt(jnp.asarray(dh, qh.dtype))
        scores = jnp.einsum('bqhe,bkhe->bhqk', qh * scale, kh)
        causal = jnp.tril(jnp.ones((BLOCK_LEN, BLOCK_LEN), bool))
        scores = jnp.where(causal, scores, NEG_INF)
        p = jax.nn.softmax(scores, axis=-1)
        o = jnp.einsum('bhqk,bkhe->bqhe', p, vh)
        o = jnp.einsum('bqhe,hed->bqd', o, wo) + bo
        o = o.reshape(N, L, W_)
        return o @ proj_w + proj_b

    def _L0_xattn_ref(hidden_states, key_value_states, attention_mask, position_bias, ln_weight, w_q, w_k, w_v, w_out):
        import jax, jax.numpy as jnp
        import numpy as np
        B, LQ, LK, D, H, DH = (2, 128, 128, 512, 32, 128)
        EPS = 1e-05

        def _rmsnorm(x, weight):
            var = jnp.mean(jnp.square(x), axis=-1, keepdims=True)
            return x * jax.lax.rsqrt(var + EPS) * weight
        x = _rmsnorm(hidden_states, ln_weight)
        b, lq, _ = x.shape
        lk = key_value_states.shape[1]
        h_q = (x @ w_q.T).reshape(b, lq, H, DH)
        h_k = (key_value_states @ w_k.T).reshape(b, lk, H, DH)
        h_v = (key_value_states @ w_v.T).reshape(b, lk, H, DH)
        score = jnp.einsum('bqhd,bkhd->bhqk', h_q, h_k)
        score = score + position_bias[None]
        m = attention_mask[:, None]
        score = jnp.where(m, score, -jnp.inf)
        score = jax.nn.softmax(score, axis=-1)
        score = jnp.where(m, score, 0.0)
        attn = jnp.einsum('bhqk,bkhd->bqhd', score, h_v).reshape(b, lq, H * DH)
        out = attn @ w_out.T
        return hidden_states + out

    def _L0_ffn_ref(x, A, B, Wr, br):
        import jax, jax.numpy as jnp
        import numpy as np
        ALPHA = 32
        R = 16
        SCALING = ALPHA / R
        H = A.shape[0]
        router_logits = jnp.einsum('bsd,hd->bsh', x, Wr) + br
        scores = H * jax.nn.softmax(router_logits, axis=-1)
        low = jnp.einsum('bsd,hrd->bshr', x, A)
        out = jnp.einsum('bshr,hor,bsh->bso', low, B, scores)
        return SCALING * out
    x = x + _L0_attn_ref(_layernorm(x, axis=-1), L0_attn_conv_w, L0_attn_conv_b, L0_attn_wq, L0_attn_bq, L0_attn_wk, L0_attn_bk, L0_attn_wv, L0_attn_bv, L0_attn_wo, L0_attn_bo, L0_attn_proj_w, L0_attn_proj_b)
    x = x + _L0_xattn_ref(_layernorm(x, axis=-1), ctx_4096, mask_BxSxS2_bk0, L0_xattn_position_bias, L0_xattn_ln_weight, L0_xattn_w_q, L0_xattn_w_k, L0_xattn_w_v, L0_xattn_w_out)
    x = x + _L0_ffn_ref(_layernorm(x, axis=-1), L0_ffn_A, L0_ffn_B, L0_ffn_Wr, L0_ffn_br)
    return x

_drawn_inputs = setup_inputs


def setup_inputs(seed=0):
    import zlib

    import numpy as np

    out = dict(_drawn_inputs(seed))
    spreads = {'L0_attn_conv_b': (0.0, 0.1),
     'L0_attn_bq': (0.0, 0.42),
     'L0_attn_bk': (0.0, 0.8),
     'L0_attn_bv': (0.0, 0.1),
     'L0_attn_bo': (0.0, 0.1),
     'L0_attn_proj_b': (0.0, 0.1),
     'L0_xattn_ln_weight': (1.0, 0.2),
     'L0_ffn_br': (0.0, 0.434)}
    factors = {}
    for name, (base, spread) in spreads.items():
        noise = np.random.default_rng([zlib.crc32(name.encode()), seed]).standard_normal(out[name].shape)
        drawn = base * np.exp(spread * noise) if base else spread * noise
        out[name] = jnp.asarray(drawn.astype(out[name].dtype))
    for name, factor in factors.items():
        out[name] = (out[name] * factor).astype(out[name].dtype)
    return out
```

```python
from contextlib import ExitStack

import concourse.bass as bass
from concourse import mybir

F32 = mybir.dt.float32
F32R = mybir.dt.float32r
BF16 = mybir.dt.bfloat16
U8 = mybir.dt.uint8
ALU = mybir.AluOpType
ACT = mybir.ActivationFunctionType
AX_X = mybir.AxisListType.X

P = 128
B = 8
D = 512
KT = D // P
TOK = B * P
HALF = TOK // 2
HB = B // 2
PAIRS = 8
ITEMS = 2 * PAIRS
XH = 32
GROUP = 4
GROUPS = XH // GROUP
E = 8
R = 16
PAD = P + 2
CONV = 3
CC = 3 * P
EPS = 1e-5
NEG = -1e9
MASKED = -1e30
BIG = 3e38
RING = 4
N_CONV = CONV * KT
WQ_AT, WO_AT, PROJ_AT, CTX_AT = N_CONV, N_CONV + 6, N_CONV + 8, N_CONV + 9
G0 = CTX_AT + 2 * KT
PER_GROUP = 4 * GROUP
SLOT = {"v": [0, 1, 2, 3], "q": [4, 6, 9, 12], "k": [5, 7, 10, 13], "o": [8, 11, 14, 15]}
ORDER = sorted((i, m, h) for m, s in SLOT.items() for h, i in enumerate(s))


def decoder_layer(nc, x, ctx_t, mask, conv_w, conv_b, wq, wk, wv, bq, bk, bv, wo, bo, proj_w, proj_b,
                  pos, lnw, xq, xk, xv, xo, aw, bw, br, out):
    with ExitStack() as ctx:
        def sb(name, shape, dt=F32):
            return ctx.enter_context(nc.sbuf_tensor(name, shape, dt))

        def sem(name):
            return ctx.enter_context(nc.semaphore(name))

        r_a = sb("r_a", [P, 8192], F32R)
        r_x = sb("r_x", [P, 2 * KT * B * PAD], F32R)
        r_c = sb("r_c", [P, 2 * N_CONV * CC], F32R)
        r_q = sb("r_q", [P, 8192], F32R)
        r_o = sb("r_o", [P, 2, HALF], F32R)
        wqkv_r = r_a[:, 0:6144].rearrange("p (s m c) -> p s m c", s=2, m=3)
        wo_r = r_a[:, 6144:8192].rearrange("p (s c) -> p s c", s=2)
        xpad_r = r_x[:, :].rearrange("p (s k b t) -> p s k b t", s=2, k=KT, b=B)
        conv_r = r_c[:, :].rearrange("p (s j c) -> p s j c", s=2, j=N_CONV)
        proj_r = r_c[:, 8192:9216].rearrange("p (s c) -> p s c", s=2)
        qkv_r = r_q[:, 0:6144].rearrange("p (s m t) -> p s m t", s=2, m=3)
        ot_r = r_q[:, 6144:8192].rearrange("p (u s t) -> p u s t", u=2, s=2)
        yt_r = r_x[:, 0:2 * TOK].rearrange("p (s t) -> p s t", s=2)
        xt_r = r_x[:, 0:2 * KT * TOK].rearrange("p (s k t) -> p s k t", s=2, k=KT)
        ct_r = r_c[:, 0:8192].rearrange("p (s k t) -> p s k t", s=2, k=KT)
        w_r = {"q": r_a[:, 0:4096], "k": r_a[:, 4096:8192], "v": r_q[:, 0:4096], "o": r_q[:, 4096:8192]}
        w_r = {m: t.rearrange("p (s h c) -> p s h c", s=2, h=GROUP) for m, t in w_r.items()}

        acc = sb("acc", [P, B, D])
        vals = sb("vals", [P, 2, HB, D])
        va = vals[:, :, :, :].rearrange("p u b c -> p (u b c)").rearrange("p (b c) -> p b c", b=HB)
        qt = sb("qt", [P, HALF])
        kt_ = sb("kt", [P, HALF])
        sc = sb("sc", [P, 2, 2, HB, P])
        hb = sc[:, :, :, :, :].rearrange("p u e b k -> p (u e) (b k)")
        scb = sc[:, 0, 0, :, :]
        pt = sb("pt", [P, 2, HALF])
        bm = sb("bm", [P, 2, HB, P])
        bmrow = bm[:, :, :, :].rearrange("p u b k -> p u (b k)")
        projb_b, lnw_b = bmrow[:, 0, :], bmrow[:, 1, :]
        maskb = sb("maskb", [P, B, P], BF16)
        mask_u = sb("mask_u", [P, B, P], U8)
        anyv = sb("anyv", [P, B])
        pb = sb("pb", [P, GROUP, P])
        ring = sb("ring", [P, RING, D])
        ident = sb("ident", [P, P])
        causal = sb("causal", [P, P])
        cb = sb("cb", [P, 3])
        bqs, bks, bvs, bos = sb("bqs", [P, PAIRS]), sb("bks", [P, PAIRS]), sb("bvs", [P, PAIRS]), sb("bos", [P, 1])
        aws = sb("aws", [P, KT, P + E])
        bws = sb("bws", [P, D])
        brs = sb("brs", [P, E])
        st = sb("st", [P, B, 6])
        mv = sb("mv", [P, B, 2])
        ve = sb("ve", [P, B])
        sd = sb("sd", [P, B])
        rs = sb("rs", [P, B])
        nt = sb("nt", [P, B])
        msq = sb("msq", [P, B])
        nmx = sb("nmx", [P, 2, 8])
        sums = sb("sums", [P, 2, 8])
        rinv = sb("rinv", [P, 8])
        scratch = sb("scratch", [P, 1])
        lg = sb("lg", [P, HB, E])
        lmx = sb("lmx", [P, HB])
        lsum = sb("lsum", [P, HB])
        lr = sb("lr", [P, HB])
        scw = sb("scw", [P, HB, E])

        bank = [ctx.enter_context(nc.psum_tensor(f"bank{i}", [P, 512], F32)) for i in range(8)]
        S2, T2, PVB, J0, J1, Y = bank[0:2], bank[2:4], bank[4], bank[5], bank[6], bank[7]
        OB, SX, TX = bank[0:4], bank[4], bank[7]

        x_ld = [sem(f"x_ld{n}") for n in range(2)]
        cst_ld, mask_ld, lnw_ld = sem("cst_ld"), sem("mask_ld"), sem("lnw_ld")
        w_ld = [sem(f"w_ld{i}") for i in range(RING)]
        pb_ld = [sem(f"pb_ld{h}") for h in range(GROUP)]
        w_hi, w_lo = sem("w_hi"), sem("w_lo")
        id_rdy, cz_rdy, pads_rdy, projb_add, mask_rdy, any_rdy = (
            sem("id_rdy"), sem("cz_rdy"), sem("pads_rdy"), sem("projb_add"), sem("mask_rdy"), sem("any_rdy"))
        ln_ve, ln_sd, xn_rdy, tp_mm, xt_hi, xt_lo, h_rdy, sq_rdy = (
            sem("ln_ve"), sem("ln_sd"), sem("xn_rdy"), sem("tp_mm"), sem("xt_hi"), sem("xt_lo"), sem("h_rdy"), sem("sq_rdy"))
        cv_mm, cv_hi, cv_lo = sem("cv_mm"), sem("cv_hi"), sem("cv_lo")
        qh_mm, kh_mm, qh_sb, kh_sb = sem("qh_mm"), sem("kh_mm"), sem("qh_sb"), sem("kh_sb")
        va_mm, va_even, va_odd = sem("va_mm"), sem("va_even"), sem("va_odd")
        s_mm, s_max, s_exp, s_rcp, s_norm = sem("s_mm"), sem("s_max"), sem("s_exp"), sem("s_rcp"), sem("s_norm")
        t_mm, pt_even, pt_odd, pv_mm, o_hi, o_lo, wo_mm, y_hi, y_lo, pj_mm, pj_add = (
            sem("t_mm"), sem("pt_even"), sem("pt_odd"), sem("pv_mm"), sem("o_hi"), sem("o_lo"), sem("wo_mm"),
            sem("y_hi"), sem("y_lo"), sem("pj_mm"), sem("pj_add"))
        xv_mm, xv_sb, xq_mm, xq_sb, xk_mm, xk_sb = (
            sem("xv_mm"), sem("xv_sb"), sem("xq_mm"), sem("xq_sb"), sem("xk_mm"), sem("xk_sb"))
        xs_mm, xs_max, xs_exp, xs_rcp, xs_norm, bm_rdy = (
            sem("xs_mm"), sem("xs_max"), sem("xs_exp"), sem("xs_rcp"), sem("xs_norm"), sem("bm_rdy"))
        xt_mm, xp_sb, xpv_mm, xo_hi, xo_lo, xo_mm, xo_add = (
            sem("xt_mm"), sem("xp_sb"), sem("xpv_mm"), sem("xo_hi"), sem("xo_lo"), sem("xo_mm"), sem("xo_add"))
        ad_mm, lg_rdy, lg_exp, g_rdy, gt_mm, gt_sb, f_mm, f_add, out_st = (
            sem("ad_mm"), sem("lg_rdy"), sem("lg_exp"), sem("g_rdy"), sem("gt_mm"), sem("gt_sb"), sem("f_mm"),
            sem("f_add"), sem("out_st"))
        dve_seq = sem("dve_seq")

        staged = []
        cw_v = conv_w.rearrange("t (k p) c -> p (t k) c", p=P)
        for j in range(N_CONV):
            staged.append((cw_v[:, j, :], conv_r[:, 0, j, :], conv_r[:, 1, j, :], CC))
        for m, w in enumerate((wq, wk, wv)):
            for s in range(2):
                c = slice(s * D, s * D + D)
                staged.append((w[:, c], wqkv_r[:, 0, m, c], wqkv_r[:, 1, m, c], D))
        wo_v = wo.rearrange("(j p) c -> p j c", p=P)
        for s in range(2):
            c = slice(s * D, s * D + D)
            staged.append((wo_v[:, 4 * s:4 * s + 4, :], wo_r[:, 0, c], wo_r[:, 1, c], D))
        staged.append((proj_w, proj_r[:, 0, :], proj_r[:, 1, :], D))
        for k in range(KT):
            for n in range(2):
                c = slice(n * HALF, n * HALF + HALF)
                staged.append((ctx_t[k * P:(k + 1) * P, c], ct_r[:, 0, k, c], ct_r[:, 1, k, c], HALF))
        assert len(staged) == G0
        xw = {"q": xq, "k": xk, "v": xv, "o": xo}

        def slot_of(pos):
            return pos % RING

        def group_item(j):
            _, m, h = ORDER[j]
            return m, h, w_r[m][:, 0, h, :], w_r[m][:, 1, h, :]

        def pos_v(first, h):
            return pos[bass.ds(first + h, 1), :, :].rearrange("a q k -> (a q) k")

        block = ctx.enter_context(nc.Block())

        @block.sync
        def _(sp):
            def load_static(pos, src, cols):
                if pos >= RING:
                    sp.wait_ge(w_lo, pos - RING + 1)
                dst = ring[:, slot_of(pos), 0:cols]
                if len(src.shape) == 3:
                    dst = dst.rearrange("p (j c) -> p j c", j=src.shape[1])
                sp.dma_start(dst, src).then_inc(w_ld[slot_of(pos)], 16)

            for pos, (src, _, _, cols) in enumerate(staged):
                load_static(pos, src, cols)
            for h in range(GROUP):
                sp.dma_start(pb[:, h, :], pos_v(0, h)).then_inc(pb_ld[h], 16)
            for j in range(PER_GROUP):
                m, h, _, _ = group_item(j)
                load_static(G0 + j, xw[m][h], D)

            with sp.Fori(0, GROUPS - 1) as g:
                for j in range(PER_GROUP):
                    m, h, _, _ = group_item(j)
                    if m == "q":
                        sp.wait_ge(bm_rdy, 8 * g + 4 + h + 1)
                        sp.dma_start(pb[:, h, :], pos_v((g + 1) * GROUP, h)).then_inc(pb_ld[h], 16)
                    pos = G0 + PER_GROUP + j
                    sp.wait_ge(w_lo, PER_GROUP * g + pos - RING + 1)
                    src = xw[m][bass.ds((g + 1) * GROUP + h, 1), :, :].rearrange("a p c -> (a p) c")
                    sp.dma_start(ring[:, slot_of(pos), :], src).then_inc(w_ld[slot_of(pos)], 16)

            for b in range(B):
                sp.wait_ge(f_add, b + 1)
                sp.dma_start(out[b], acc[:, b, :]).then_inc(out_st, 16)
            sp.wait_ge(out_st, 16 * B)

        @block.gpsimd
        def _(pool):
            def split_hi(pos, dst, cols):
                pool.wait_ge(w_ld[slot_of(pos)], 16 * (pos // RING + 1))
                nc.gpsimd.tensor_copy(dst, ring[:, slot_of(pos), 0:cols]).then_inc(w_hi, 1)

            nc.gpsimd.memset(ident[:], 0.0).then_inc(cz_rdy, 1)
            nc.gpsimd.memset(causal[:], 0.0).then_inc(cz_rdy, 1)
            nc.gpsimd.memset(xpad_r[:, :, :, :, 0:PAD:PAD - 1].bitcast(F32)
                             .rearrange("p s k b t -> p (s k b) t"), 0.0).then_inc(pads_rdy, 1)
            pool.wait_ge(cz_rdy, 2)
            nc.gpsimd.affine_select(out=ident[:], in_=ident[:], compare_op=ALU.not_equal, fill=1.0, base=0,
                                    pattern=[[-1, P]], channel_multiplier=1).then_inc(id_rdy, 1)
            nc.gpsimd.affine_select(out=causal[:], in_=causal[:], compare_op=ALU.is_ge, fill=NEG, base=0,
                                    pattern=[[-1, P]], channel_multiplier=1).then_inc(id_rdy, 1)
            for p_ in range(WO_AT + 2):
                _, hi, _, cols = staged[p_]
                split_hi(p_, hi, cols)
            pool.wait_ge(cst_ld, 16 * N_CST)
            for n in range(2):
                pool.wait_ge(xn_rdy, HB * (n + 1))
                for b in range(HB * n, HB * n + HB):
                    nc.gpsimd.tensor_tensor(acc[:, b, :], acc[:, b, :], projb_b, ALU.add).then_inc(projb_add, 1)
            pool.wait_ge(mask_ld, 16)
            nc.gpsimd.tensor_scalar(maskb[:, :, :], mask_u[:, :, :], 1.0, -MASKED, ALU.subtract, ALU.mult)\
                .then_inc(mask_rdy, 1)
            pool.wait_ge(cv_mm, 6)
            for p_ in range(PROJ_AT, G0):
                _, hi, _, cols = staged[p_]
                split_hi(p_, hi, cols)

            def first_group():
                for j in range(PER_GROUP):
                    m, h, hi, _ = group_item(j)
                    if j == 0:
                        pool.wait_ge(kh_mm, ITEMS)
                        pool.wait_ge(va_mm, 2 * B)
                    if j == 4:
                        pool.wait_ge(wo_mm, ITEMS)
                    split_hi(G0 + j, hi, D)

            def bias_mask(c, q):
                h, n = q % GROUP, q // GROUP % 2
                pool.wait_ge(pb_ld[h], 16 * c[1] + 16)
                nc.gpsimd.tensor_tensor(bm[:, q % 2, :, :], maskb[:, HB * n:HB * n + HB, :],
                                        pb[:, h, :].unsqueeze(1).broadcast_to((P, HB, P)), ALU.add)\
                    .then_inc(bm_rdy, 1)

            first_group()
            pool.wait_ge(mask_rdy, 1)
            pool.wait_ge(xn_rdy, 2 * B)
            bias_mask((0, 0), 0)
            bias_mask((1, 0), 1)

            def group(g, last):
                for q in range(1, 9):
                    c = 8 * g + q
                    if not last or q < 7:
                        pool.wait_ge(xs_max, 4 * c)
                        bias_mask((c + 1, g + (q + 1) // 8), (q + 1) % 8)

            with pool.Fori(0, GROUPS - 1) as g:
                group(g, False)
            group(GROUPS - 1, True)

        @block.scalar
        def _(act):
            xv_ = x.rearrange("b t d -> t b d")
            for n in range(2):
                act.dma_start(acc[:, HB * n:HB * n + HB, :], xv_[:, HB * n:HB * n + HB, :]).then_inc(x_ld[n], 16)
            small = [(cb[:], conv_b), (bqs[:], bq), (bks[:], bk), (bvs[:], bv), (bos[:], bo),
                     (projb_b, proj_b.partition_broadcast(P)), (aws[:, :, :], aw.rearrange("(k p) c -> p k c", p=P)),
                     (bws[:], bw), (brs[:], br.partition_broadcast(P))]
            assert len(small) == N_CST
            for dst, src in small:
                act.dma_start(dst, src).then_inc(cst_ld, 16)
            act.dma_start(lnw_b, lnw.partition_broadcast(P)).then_inc(lnw_ld, 16)
            act.dma_start(mask_u[:, :, :], mask.rearrange("b q k -> q b k")).then_inc(mask_ld, 16)

            def root(i, col):
                act.wait_ge(ln_ve, i + 1)
                nc.scalar.activation(sd[:, col:col + HB], ve[:, col:col + HB], ACT.Sqrt).then_inc(ln_sd, 1)

            for n in range(2):
                root(n, HB * n)
                for b in range(HB * n, HB * n + HB):
                    act.wait_ge(tp_mm, b + 1)
                    nc.scalar.activation(xpad_r[:, 0, :, b, 1:1 + P],
                                         bank[b % 2][:, :].rearrange("p (k t) -> p k t", k=KT), ACT.Copy)\
                        .then_inc(xt_hi, 1)
            act.wait_ge(cst_ld, 16 * N_CST)
            for j in range(6):
                n, m = divmod(j, 3)
                act.wait_ge(cv_mm, j + 1)
                nc.scalar.activation(qkv_r[:, 0, m, n * HALF:(n + 1) * HALF], bank[2 + j][:, :], ACT.Identity,
                                     bias=cb[:, m:m + 1]).then_inc(cv_hi, 1)

            def kh_out(i):
                act.wait_ge(kh_mm, i + 1)
                nc.scalar.activation(kt_[:], J1[:, :], ACT.Identity, bias=bks[:, i % PAIRS:i % PAIRS + 1])\
                    .then_inc(kh_sb, 1)

            kh_out(0)
            for i in range(ITEMS + 2):
                for e in range(2):
                    if i < ITEMS:
                        for b in range(HB):
                            k = 4 * e + b
                            act.wait_ge(s_max, 8 * i + k + 1)
                            t = sc[:, i % 2, e, b, :]
                            nc.scalar.activation(t, t, ACT.Exp, scale=-1.0, bias=nmx[:, i % 2, k:k + 1],
                                                 accum_out=sums[:, i % 2, k:k + 1]).then_inc(s_exp, 1)
                    if e == 0 and 1 <= i <= ITEMS:
                        act.wait_ge(t_mm, i)
                        nc.scalar.copy(pt[:, 0, :], T2[0][:, :]).then_inc(pt_even, 1)
                if i + 1 < ITEMS:
                    kh_out(i + 1)
                if i - 2 in (PAIRS - 1, ITEMS - 1):
                    n = (i - 2) // PAIRS
                    act.wait_ge(wo_mm, i - 1)
                    nc.scalar.activation(yt_r[:, 0, n * HALF:(n + 1) * HALF], Y[:, :], ACT.Identity,
                                         bias=bos[:, 0:1]).then_inc(y_hi, 1)
                if 1 <= i <= ITEMS:
                    act.wait_ge(pv_mm, i)
                    p_ = (i - 1) % PAIRS
                    nc.scalar.activation(ot_r[:, (i - 1) % 2, 0, :], PVB[:, :], ACT.Identity,
                                         bias=bvs[:, p_:p_ + 1]).then_inc(o_hi, 1)
                if i % PAIRS == 0 and i < ITEMS:
                    for m in range(0, B, 2):
                        act.wait_ge(va_mm, i + m + 1)
                        nc.scalar.copy(va[:, m // 2, 0:D], J0[:, :]).then_inc(va_even, 1)

            for b in range(HB):
                act.wait_ge(xv_mm, b + 1)
                nc.scalar.copy(vals[:, 0, b, :], (J0, J1)[b % 2][:, :]).then_inc(xv_sb, 1)

            for n in range(2):
                root(2 + 2 * n, HB * n)
                for j in range(HB):
                    b = HB * n + j
                    act.wait_ge(h_rdy, b + 1)
                    nc.scalar.activation((pt[:, 0, :], pt[:, 1, :], qt[:], kt_[:])[j], hb[:, j, :], ACT.Square, accum_out=msq[:, b:b + 1])\
                        .then_inc(sq_rdy, 1)
                root(3 + 2 * n, HB * n)
                for j in range(HB):
                    b = HB * n + j
                    act.wait_ge(tp_mm, B + b + 1)
                    nc.scalar.activation(xt_r[:, 0, :, b * P:(b + 1) * P],
                                         bank[b % 2][:, :].rearrange("p (k t) -> p k t", k=KT), ACT.Copy)\
                        .then_inc(xt_hi, 1)

            def quarter(c, q, back, front):
                if front:
                    act.wait_ge(xq_mm, c + 1)
                    nc.scalar.copy(qt[:], J0[:, :]).then_inc(xq_sb, 1)
                if back:
                    act.wait_ge(xt_mm, c)
                    nc.scalar.copy(pt[:, 0, :], TX[:, :]).then_inc(xp_sb, 1)
                if front:
                    act.wait_ge(xk_mm, c + 1)
                    nc.scalar.copy(kt_[:], J1[:, :]).then_inc(xk_sb, 1)
                if back:
                    act.wait_ge(xpv_mm, c)
                    nc.scalar.activation(r_o[:, 0, :], TX[:, :], ACT.Copy).then_inc(xo_hi, 1)
                if front:
                    for b in range(HB):
                        act.wait_ge(xs_max, 4 * c + b + 1)
                        t = scb[:, b, :]
                        nc.scalar.activation(t, t, ACT.Exp, scale=-1.0, bias=nmx[:, 0, b:b + 1],
                                             accum_out=sums[:, 0, b:b + 1]).then_inc(xs_exp, 1)
                    if front != "last":
                        act.wait_ge(xv_mm, c + 5)
                        u = (q // GROUP + 1) % 2
                        nc.scalar.copy(vals[:, u, q % GROUP, :], J0[:, :]).then_inc(xv_sb, 1)

            quarter(0, 0, False, True)
            with act.Fori(0, GROUPS - 1) as g:
                for q in range(1, 9):
                    quarter(8 * g + q, q, True, True)
            for q in range(1, 9):
                quarter(8 * (GROUPS - 1) + q, q, True, False if q == 8 else "last" if q >= 4 else True)

            for n in range(2):
                root(6 + n, HB * n)
                for j in range(HB):
                    b = HB * n + j
                    act.wait_ge(tp_mm, 2 * B + b + 1)
                    if b >= 2:
                        act.wait_ge(ad_mm, b - 1)
                    nc.scalar.copy(pt[:, b % 2, :], bank[b % 2][:, :]).then_inc(xt_hi, 1)
                act.wait_ge(lg_rdy, n + 1)
                nc.scalar.activation(lg[:, :, :], lg[:, :, :], ACT.Exp).then_inc(lg_exp, 1)
                act.wait_ge(gt_mm, n + 1)
                if n:
                    act.wait_ge(f_mm, HB)
                nc.scalar.copy(kt_[:], bank[4][:, :]).then_inc(gt_sb, 1)

        @block.vector
        def _(dve):
            done = [0]

            def link(ins):
                done[0] += 1
                ins.then_inc(dve_seq, 1)
                dve.wait_ge(dve_seq, done[0])

            def split_lo(pos, base, hi, lo, cols):
                dve.wait_ge(w_hi, base + pos + 1)
                nc.vector.tensor_tensor(lo, ring[:, slot_of(pos), 0:cols], hi.bitcast(F32), ALU.subtract)\
                    .then_inc(w_lo, 1)

            def split_static(a, z):
                for p_ in range(a, z):
                    if p_ < G0:
                        _, hi, lo, cols = staged[p_]
                        split_lo(p_, 0, hi, lo, cols)
                    else:
                        _, _, hi, lo = group_item(p_ - G0)
                        split_lo(p_, 0, hi, lo, D)

            def rsqrt(i, cols):
                v, s, r, t = ve[:, cols], sd[:, cols], rs[:, cols], nt[:, cols]
                dve.wait_ge(ln_sd, i + 1)
                link(nc.vector.reciprocal(r, s))
                link(nc.vector.tensor_tensor(t, r, r, ALU.mult))
                link(nc.vector.tensor_tensor(t, t, v, ALU.mult))
                link(nc.vector.tensor_scalar(t, t, -0.5, 1.5, ALU.mult, ALU.add))
                link(nc.vector.tensor_tensor(r, r, t, ALU.mult))

            def moments(i, n):
                for b in range(HB * n, HB * n + HB):
                    ins = nc.vector.bn_stats(st[:, b, :], acc[:, b, :])
                link(ins)
                for b in range(HB * n, HB * n + HB):
                    ins = nc.vector.bn_aggr(mv[:, b, :], st[:, b, :])
                link(ins)
                cols = slice(HB * n, HB * n + HB)
                nc.vector.tensor_scalar(ve[:, cols], mv[:, cols, 1], EPS, None, ALU.add).then_inc(ln_ve, 1)
                rsqrt(i, cols)

            def centre(dst, b):
                return nc.vector.tensor_scalar(dst, acc[:, b, :], mv[:, b, 0:1], rs[:, b:b + 1],
                                               ALU.subtract, ALU.mult)

            def tile_lo(k, dst, hi):
                dve.wait_ge(xt_hi, k + 1)
                src = bank[k % 2][:, :].rearrange("p (k t) -> p k t", k=KT)
                nc.vector.tensor_tensor(dst, src, hi.bitcast(F32), ALU.subtract).then_inc(xt_lo, 1)

            split_static(0, RING)
            dve.wait_ge(pads_rdy, 1)
            for n in range(2):
                dve.wait_ge(x_ld[n], 16)
                moments(n, n)
                for b in range(HB * n, HB * n + HB + 1):
                    if b < HB * n + HB:
                        if b >= 2:
                            dve.wait_ge(tp_mm, b - 1)
                        centre(pt[:, b % 2, :], b).then_inc(xn_rdy, 1)
                    if b > HB * n:
                        tile_lo(b - 1, xpad_r[:, 1, :, b - 1, 1:1 + P], xpad_r[:, 0, :, b - 1, 1:1 + P])
                if n == 0:
                    split_static(RING, N_CONV)
            split_static(N_CONV, WO_AT)
            dve.wait_ge(cst_ld, 16 * N_CST)
            for j in range(6):
                n, m = divmod(j, 3)
                t = slice(n * HALF, (n + 1) * HALF)
                dve.wait_ge(cv_hi, j + 1)
                nc.vector.scalar_tensor_tensor(qkv_r[:, 1, m, t], bank[2 + j][:, :], cb[:, m:m + 1],
                                               qkv_r[:, 0, m, t].bitcast(F32), ALU.add, ALU.subtract)\
                    .then_inc(cv_lo, 1)
            split_static(WO_AT, WO_AT + 2)

            def qh_out(i):
                dve.wait_ge(qh_mm, i + 1)
                nc.vector.tensor_scalar(qt[:], J0[:, :], bqs[:, i % PAIRS:i % PAIRS + 1], 0.125,
                                        ALU.add, ALU.mult).then_inc(qh_sb, 1)

            qh_out(0)
            dve.wait_ge(id_rdy, 2)
            for i in range(ITEMS + 2):
                if i < ITEMS:
                    dve.wait_ge(s_mm, i + 1)
                    for k in range(8):
                        e, b = divmod(k, HB)
                        nc.vector.tensor_tensor_reduce(
                            sc[:, i % 2, e, b, :], S2[e][:, b * P:(b + 1) * P], causal[:], -1.0, BIG,
                            ALU.add, ALU.min, nmx[:, i % 2, k:k + 1]).then_inc(s_max, 1)
                if 1 <= i <= ITEMS:
                    dve.wait_ge(t_mm, i)
                    nc.vector.tensor_copy(pt[:, 1, :], T2[1][:, :]).then_inc(pt_odd, 1)
                if i + 1 < ITEMS:
                    qh_out(i + 1)
                if 1 <= i <= G0 - PROJ_AT:
                    split_static(PROJ_AT + i - 1, PROJ_AT + i)
                if i < ITEMS:
                    dve.wait_ge(s_exp, 8 * i + 8)
                    nc.vector.reciprocal(rinv[:], sums[:, i % 2, :]).then_inc(s_rcp, 1)
                    dve.wait_ge(s_rcp, i + 1)
                    t = sc[:, i % 2, :, :, :].rearrange("p e b k -> p (e b) k")
                    nc.vector.tensor_tensor(t, t, rinv[:].unsqueeze(2).broadcast_to((P, 8, P)), ALU.mult)\
                        .then_inc(s_norm, 1)
                if i - 2 in (PAIRS - 1, ITEMS - 1):
                    n = (i - 2) // PAIRS
                    t = slice(n * HALF, (n + 1) * HALF)
                    dve.wait_ge(y_hi, n + 1)
                    nc.vector.scalar_tensor_tensor(yt_r[:, 1, t], Y[:, :], bos[:, 0:1],
                                                   yt_r[:, 0, t].bitcast(F32), ALU.add, ALU.subtract)\
                        .then_inc(y_lo, 1)
                if 1 <= i <= ITEMS:
                    p_, u = (i - 1) % PAIRS, (i - 1) % 2
                    dve.wait_ge(o_hi, i)
                    nc.vector.scalar_tensor_tensor(ot_r[:, u, 1, :], PVB[:, :], bvs[:, p_:p_ + 1],
                                                   ot_r[:, u, 0, :].bitcast(F32), ALU.add, ALU.subtract)\
                        .then_inc(o_lo, 1)
                if i % PAIRS == 0 and i < ITEMS:
                    for m in range(1, B, 2):
                        dve.wait_ge(va_mm, i + m + 1)
                        nc.vector.tensor_copy(va[:, m // 2, D:2 * D], J1[:, :]).then_inc(va_odd, 1)
            split_static(G0, G0 + GROUP)

            dve.wait_ge(projb_add, B)
            for b in range(B):
                dve.wait_ge(pj_mm, b + 1)
                nc.vector.tensor_tensor(acc[:, b, :], acc[:, b, :], bank[b % 4][:, :], ALU.add).then_inc(pj_add, 1)
            dve.wait_ge(pj_add, B)

            dve.wait_ge(lnw_ld, 16)
            for n in range(2):
                cols = slice(HB * n, HB * n + HB)
                moments(2 + 2 * n, n)
                for j in range(HB):
                    b = HB * n + j
                    if n:
                        dve.wait_ge(tp_mm, B + j + 1)
                    centre(hb[:, j, :], b).then_inc(h_rdy, 1)
                for j in range(HB):
                    b = HB * n + j
                    dve.wait_ge(h_rdy, b + 1)
                    nc.vector.tensor_tensor(acc[:, b, :], acc[:, b, :], hb[:, j, :], ALU.add).then_inc(xo_add, 1)
                dve.wait_ge(sq_rdy, HB * (n + 1))
                nc.vector.tensor_scalar(ve[:, cols], msq[:, cols], 1.0 / D, EPS, ALU.mult, ALU.add).then_inc(ln_ve, 1)
                rsqrt(3 + 2 * n, cols)
                for j in range(HB):
                    b = HB * n + j
                    nc.vector.scalar_tensor_tensor(hb[:, j, :], hb[:, j, :], rs[:, b:b + 1], lnw_b,
                                                   ALU.mult, ALU.mult).then_inc(xn_rdy, 1)
                for j in range(HB):
                    b = HB * n + j
                    t = slice(b * P, (b + 1) * P)
                    tile_lo(B + b, xt_r[:, 1, :, t], xt_r[:, 0, :, t])
                if n == 0:
                    split_static(G0 + 4, G0 + 6)
            split_static(G0 + 6, G0 + PER_GROUP)
            dve.wait_ge(mask_ld, 16)
            nc.vector.tensor_reduce(anyv[:], mask_u[:, :, :], AX_X, ALU.max).then_inc(any_rdy, 1)
            dve.wait_ge(any_rdy, 1)

            def quarter(c, q, back, front):
                if back:
                    dve.wait_ge(xo_hi, c)
                    nc.vector.tensor_tensor(r_o[:, 1, :], TX[:, :], r_o[:, 0, :].bitcast(F32), ALU.subtract)\
                        .then_inc(xo_lo, 1)
                if front:
                    n = q // GROUP % 2
                    dve.wait_ge(xs_mm, c + 1)
                    dve.wait_ge(bm_rdy, c + 1)
                    nc.vector.memset(scratch[:], 0.0)
                    for b in range(HB):
                        nc.vector.tensor_tensor_reduce(
                            scb[:, b, :], SX[:, b * P:(b + 1) * P], bm[:, q % 2, b, :], -1.0, BIG,
                            ALU.add, ALU.min, nmx[:, 0, b:b + 1]).then_inc(xs_max, 1)
                    dve.wait_ge(xs_exp, 4 * c + 4)
                    nc.vector.reciprocal(rinv[:, 0:HB], sums[:, 0, 0:HB]).then_inc(xs_rcp, 1)
                    dve.wait_ge(xs_rcp, 2 * c + 1)
                    nc.vector.tensor_tensor(rinv[:, 0:HB], rinv[:, 0:HB], anyv[:, HB * n:HB * n + HB], ALU.mult)\
                        .then_inc(xs_rcp, 1)
                    dve.wait_ge(xs_rcp, 2 * c + 2)
                    nc.vector.tensor_tensor(scb, scb, rinv[:, 0:HB].unsqueeze(2).broadcast_to((P, HB, P)), ALU.mult)\
                        .then_inc(xs_norm, 1)

            def add_out(c, n):
                dve.wait_ge(xo_mm, c)
                for b in range(HB):
                    a = acc[:, HB * n + b, :]
                    nc.vector.tensor_tensor(a, a, OB[b][:, :], ALU.add).then_inc(xo_add, 1)

            quarter(0, 0, False, True)
            with dve.Fori(0, GROUPS - 1) as g:
                base = PER_GROUP * g

                def split(m, s):
                    j = SLOT[m][s]
                    pos = G0 + PER_GROUP + j
                    _, _, hi, low = group_item(j)
                    dve.wait_ge(w_ld[slot_of(pos)], 16 * (pos // RING + 1) + PER_GROUP // RING * 16 * g)
                    nc.vector.tensor_copy(hi, ring[:, slot_of(pos), :]).then_inc(w_hi, 1)
                    split_lo(pos, base, hi, low, D)

                for q in range(1, 9):
                    c = 8 * g + q
                    h = q - GROUP
                    if q == 4:
                        dve.wait_ge(xv_mm, c + 4)
                        for s in range(GROUP):
                            split("v", s)
                    quarter(c, q, True, True)
                    if 4 <= q < 8:
                        dve.wait_ge(xk_mm, c + 1)
                        split("q", h)
                        split("k", h)
                    if q % GROUP == 0:
                        add_out(c, q // GROUP - 1)
                    if 5 <= q:
                        dve.wait_ge(xo_mm, c)
                        split("o", h - 1)
            for q in range(1, 9):
                c = 8 * (GROUPS - 1) + q
                quarter(c, q, True, q < 8)
                if q % GROUP == 0:
                    add_out(c, q // GROUP - 1)
            dve.wait_ge(xo_add, B + B * GROUPS)

            for n in range(2):
                moments(6 + n, n)
                for j in range(HB):
                    b = HB * n + j
                    if n:
                        dve.wait_ge(tp_mm, 2 * B + j + 1)
                    centre(hb[:, j, :], b).then_inc(xn_rdy, 1)
                dve.wait_ge(ad_mm, HB * (n + 1))
                link(nc.vector.tensor_tensor(lg[:, :, :], bank[3][:, 0:HB * E].rearrange("p (b e) -> p b e", b=HB),
                                             brs[:].unsqueeze(1).broadcast_to((P, HB, E)), ALU.add))
                link(nc.vector.tensor_reduce(lmx[:], lg[:, :, :], AX_X, ALU.max))
                nc.vector.tensor_tensor(lg[:, :, :], lg[:, :, :], lmx[:].unsqueeze(2).broadcast_to((P, HB, E)),
                                        ALU.subtract).then_inc(lg_rdy, 1)
                dve.wait_ge(lg_exp, n + 1)
                link(nc.vector.tensor_reduce(lsum[:], lg[:, :, :], AX_X, ALU.add))
                link(nc.vector.reciprocal(lr[:], lsum[:]))
                link(nc.vector.tensor_scalar(lr[:], lr[:], 2.0 * E, None, ALU.mult))
                link(nc.vector.tensor_tensor(scw[:, :, :], lg[:, :, :], lr[:].unsqueeze(2).broadcast_to((P, HB, E)),
                                             ALU.mult))
                gates = scw[:, :, :].rearrange("p b e -> p (b e)").unsqueeze(2).broadcast_to((P, HB * E, R))
                nc.vector.tensor_tensor(bmrow[:, n, :].rearrange("p (m r) -> p m r", r=R),
                                        bank[2][:, :].rearrange("p (m r) -> p m r", r=R), gates, ALU.mult)\
                    .then_inc(g_rdy, 1)
                for j in range(HB):
                    b = HB * n + j
                    dve.wait_ge(f_mm, b + 1)
                    nc.vector.tensor_tensor(acc[:, b, :], acc[:, b, :], bank[5 + b % 3][:, :], ALU.add)\
                        .then_inc(f_add, 1)

        @block.tensor
        def _(pe):
            def three(dst, a, w, first=True, last=True):
                nc.tensor.matmul(dst, a(0), w(0), start=first, stop=False)
                nc.tensor.matmul(dst, a(1), w(0), start=False, stop=False)
                return nc.tensor.matmul(dst, a(0), w(1), start=False, stop=last)

            def tile_turn(k, src, free):
                pe.wait_ge(xn_rdy, k + 1)
                if free is not None:
                    pe.wait_ge(*free)
                for kt in range(KT):
                    ins = nc.tensor.transpose(bank[k % 2][:, kt * P:(kt + 1) * P], src[:, kt * P:(kt + 1) * P], ident[:])
                ins.then_inc(tp_mm, 1)

            pe.wait_ge(id_rdy, 2)
            for n in range(2):
                for b in range(HB * n, HB * n + HB):
                    tile_turn(b, pt[:, b % 2, :], (xt_lo, b - 1) if b >= 2 else None)
                for m in range(3):
                    if m == 0:
                        pe.wait_ge(xt_lo, HB * (n + 1))
                    for j in range(N_CONV):
                        t, kt = divmod(j, KT)
                        if m == 0 and n == 0:
                            pe.wait_ge(w_lo, j + 1)
                        ins = three(bank[2 + 3 * n + m][:, :].rearrange("p (b t) -> p b t", b=HB),
                                    lambda s: conv_r[:, s, j, m * P:(m + 1) * P],
                                    lambda s: xpad_r[:, s, kt, HB * n:HB * n + HB, t:t + P],
                                    j == 0, j == N_CONV - 1)
                    ins.then_inc(cv_mm, 1)

            def head_proj(i, m, dst, done):
                n, p_ = divmod(i, PAIRS)
                three(dst, lambda s: wqkv_r[:, s, m, p_ * P:(p_ + 1) * P],
                      lambda s: qkv_r[:, s, m, n * HALF:(n + 1) * HALF]).then_inc(done, 1)

            pe.wait_ge(cv_lo, 6)
            pe.wait_ge(w_lo, WO_AT)
            head_proj(0, 0, J0[:, :], qh_mm)
            head_proj(0, 1, J1[:, :], kh_mm)
            for i in range(ITEMS + 2):
                if i < ITEMS:
                    pe.wait_ge(qh_sb, i + 1)
                    pe.wait_ge(kh_sb, i + 1)
                    if i:
                        pe.wait_ge(s_max, 8 * i)
                    for b in range(HB):
                        for e in range(2):
                            t, h = slice(b * P, (b + 1) * P), slice(64 * e, 64 * e + 64)
                            ins = nc.tensor.matmul(S2[e][:, t], qt[h, t], kt_[h, t], start=True, stop=True)
                    ins.then_inc(s_mm, 1)
                if 1 <= i <= ITEMS:
                    pe.wait_ge(s_norm, i)
                    for e in range(2):
                        for b in range(HB):
                            ins = nc.tensor.transpose(T2[e][:, b * P:(b + 1) * P], sc[:, (i - 1) % 2, e, b, :], ident[:])
                    ins.then_inc(t_mm, 1)
                if i + 1 < ITEMS:
                    if i >= 1:
                        pe.wait_ge(va_even, HB * ((i - 1) // PAIRS + 1))
                        pe.wait_ge(va_odd, HB * ((i - 1) // PAIRS + 1))
                    head_proj(i + 1, 0, J0[:, :], qh_mm)
                    head_proj(i + 1, 1, J1[:, :], kh_mm)
                if i >= 2:
                    p_, u = (i - 2) % PAIRS, i % 2
                    pe.wait_ge(o_lo, i - 1)
                    if i == 2:
                        pe.wait_ge(w_lo, WO_AT + 2)
                    if i - 2 == PAIRS:
                        pe.wait_ge(y_lo, 1)
                    three(Y[:, :], lambda s: wo_r[:, s, p_ * P:(p_ + 1) * P], lambda s: ot_r[:, u, s, :],
                          p_ == 0, p_ == PAIRS - 1).then_inc(wo_mm, 1)
                if 1 <= i <= ITEMS:
                    p_ = (i - 1) % PAIRS
                    pe.wait_ge(pt_even, i)
                    pe.wait_ge(pt_odd, i)
                    for b in range(HB):
                        for e in range(2):
                            ins = nc.tensor.matmul(PVB[64 * e:64 * e + 64, b * P:(b + 1) * P],
                                                   va[:, b, p_ * P + 64 * e:p_ * P + 64 * e + 64],
                                                   pt[:, e, b * P:(b + 1) * P], start=True, stop=True)
                    ins.then_inc(pv_mm, 1)
                if i % PAIRS == 0 and i < ITEMS:
                    n = i // PAIRS
                    for m in range(B):
                        if m < 2:
                            pe.wait_ge((qh_sb, kh_sb)[m], i + 2)
                        else:
                            pe.wait_ge((va_even, va_odd)[m % 2], HB * n + m // 2)
                        b = HB * n + m // 2
                        three((J0, J1)[m % 2][:, :], lambda s: qkv_r[:, s, 2, b * P:(b + 1) * P],
                              lambda s: wqkv_r[:, s, 2, m % 2 * D:(m % 2 + 1) * D]).then_inc(va_mm, 1)
            pe.wait_ge(y_lo, 2)
            pe.wait_ge(w_lo, PROJ_AT + 1)
            for b in range(B):
                if b >= 4:
                    pe.wait_ge(pj_add, b - 3)
                three(bank[b % 4][:, :], lambda s: yt_r[:, s, b * P:(b + 1) * P], lambda s: proj_r[:, s, :])\
                    .then_inc(pj_mm, 1)

            def xproj(dst, m, h, n):
                src = xt_r if m == "q" else ct_r
                for kt in range(KT):
                    ins = three(dst, lambda s: w_r[m][:, s, h, kt * P:(kt + 1) * P],
                                lambda s: src[:, s, kt, n * HALF:(n + 1) * HALF], kt == 0, kt == KT - 1)
                return ins

            def xvalues(dst, b):
                for kt in range(KT):
                    ins = three(dst, lambda s: ct_r[:, s, kt, b * P:(b + 1) * P],
                                lambda s: w_r["v"][:, s, kt, :], kt == 0, kt == KT - 1)
                ins.then_inc(xv_mm, 1)

            pe.wait_ge(w_lo, G0 + GROUP)
            for b in range(HB):
                if b >= 2:
                    pe.wait_ge(xv_sb, b - 1)
                xvalues((J0, J1)[b % 2][:, :], b)
            for k in range(B, 2 * B):
                tile_turn(k, hb[:, k % HB, :], (xt_lo, k - 1) if k >= B + 2 else (pj_add, B))

            def quarter(c, q, back, front):
                h, n = q % GROUP, q // GROUP % 2
                hp, np_ = (q - 1) % GROUP, (q - 1) // GROUP % 2
                if front:
                    if front != "last" or q == GROUP:
                        pe.wait_ge(xv_sb, c + 4)
                    xproj(J0[:, :], "q", h, n).then_inc(xq_mm, 1)
                if back:
                    pe.wait_ge(xs_norm, c)
                    for b in range(HB):
                        ins = nc.tensor.transpose(TX[:, b * P:(b + 1) * P], scb[:, b, :], ident[:])
                    ins.then_inc(xt_mm, 1)
                if front:
                    xproj(J1[:, :], "k", h, n).then_inc(xk_mm, 1)
                if back:
                    pe.wait_ge(xp_sb, c)
                    for b in range(HB):
                        t = slice(b * P, (b + 1) * P)
                        ins = nc.tensor.matmul(TX[:, t], vals[:, np_, b, hp * P:(hp + 1) * P], pt[:, 0, t],
                                               start=True, stop=True)
                    ins.then_inc(xpv_mm, 1)
                if front:
                    pe.wait_ge(xq_sb, c + 1)
                    pe.wait_ge(xk_sb, c + 1)
                    for b in range(HB):
                        t = slice(b * P, (b + 1) * P)
                        ins = nc.tensor.matmul(SX[:, t], qt[:, t], kt_[:, t], start=True, stop=True)
                    ins.then_inc(xs_mm, 1)
                    if front != "last":
                        xvalues(J0[:, :], HB * (1 - n) + h)
                if back:
                    pe.wait_ge(xo_lo, c)
                    for b in range(HB):
                        ins = three(OB[b][:, :], lambda s: r_o[:, s, b * P:(b + 1) * P],
                                    lambda s: w_r["o"][:, s, hp, :], hp == 0, hp == GROUP - 1)
                    ins.then_inc(xo_mm, 1)

            pe.wait_ge(w_lo, G0 + PER_GROUP)
            pe.wait_ge(xt_lo, 2 * B)
            quarter(0, 0, False, True)

            def group(g, last):
                for q in range(1, 9):
                    c = 8 * g + q
                    at = PER_GROUP * g + G0
                    h = q % GROUP
                    if q < GROUP:
                        pe.wait_ge(w_lo, at + SLOT["k"][h] + 1)
                    if q == GROUP and not last:
                        pe.wait_ge(w_lo, at + PER_GROUP + GROUP)
                    if q == 8 and not last:
                        pe.wait_ge(w_lo, at + PER_GROUP + SLOT["k"][0] + 1)
                    if q <= GROUP:
                        pe.wait_ge(w_lo, at + SLOT["o"][q - 1] + 1)
                    if q % GROUP == 1:
                        pe.wait_ge(xo_add, B * g + B + HB * (q // GROUP))
                    quarter(c, q, True, False if last and q == 8 else "last" if last and q >= 4 else True)
            with pe.Fori(0, GROUPS - 1) as g:
                group(g, False)
            group(GROUPS - 1, True)

            def adapt(b):
                j = b % HB
                pe.wait_ge(xt_hi, 2 * B + b + 1)
                if j == 0 and b:
                    pe.wait_ge(g_rdy, 1)
                for kt in range(KT):
                    nc.tensor.matmul(bank[2][:, j * P:(j + 1) * P], pt[:, b % 2, kt * P:(kt + 1) * P],
                                     aws[:, kt, 0:P], start=kt == 0, stop=kt == KT - 1)
                for kt in range(KT):
                    ins = nc.tensor.matmul(bank[3][:, j * E:(j + 1) * E], pt[:, b % 2, kt * P:(kt + 1) * P],
                                           aws[:, kt, P:P + E], start=kt == 0, stop=kt == KT - 1)
                ins.then_inc(ad_mm, 1)

            for n in range(2):
                for j in range(HB + 1):
                    b = HB * n + j
                    if j < HB:
                        tile_turn(2 * B + b, hb[:, j, :], (xt_hi, 2 * B + b - 1) if b >= 2 else None)
                    if j:
                        adapt(b - 1)
                pe.wait_ge(g_rdy, n + 1)
                for j in range(HB):
                    ins = nc.tensor.transpose(bank[4][:, j * P:(j + 1) * P], bmrow[:, n, j * P:(j + 1) * P], ident[:])
                ins.then_inc(gt_mm, 1)
                pe.wait_ge(gt_sb, n + 1)
                for j in range(HB):
                    b = HB * n + j
                    if b >= 3:
                        pe.wait_ge(f_add, b - 2)
                    nc.tensor.matmul(bank[5 + b % 3][:, :], kt_[:, j * P:(j + 1) * P], bws[:], start=True, stop=True)\
                        .then_inc(f_mm, 1)


N_CST = 9


def kernel(**inputs):
    import numpy as _np
    import concourse.bacc as _bacc
    from concourse import mybir as _mybir
    from concourse.bass_utils import run_bass_kernel_spmd as _run

    a = {k.replace("L0_", ""): _np.asarray(v) for k, v in inputs.items()}

    def heads(w):
        return w.reshape(XH, P, KT, P).transpose(0, 3, 2, 1).reshape(XH, P, D)

    xv = a["xattn_w_v"].reshape(GROUPS, D, KT, P).transpose(0, 2, 3, 1).reshape(XH, P, D)
    layout = {
        "x": a["x"],
        "ctx_t": a["ctx_4096"].reshape(TOK, D).T,
        "mask": a["mask_BxSxS2_bk0"],
        "conv_w": a["attn_conv_w"],
        "conv_b": a["attn_conv_b"].reshape(3, P).T,
        "wq": a["attn_wq"].reshape(P, 2 * D), "wk": a["attn_wk"].reshape(P, 2 * D), "wv": a["attn_wv"].reshape(P, 2 * D),
        "bq": a["attn_bq"].reshape(PAIRS, P).T, "bk": a["attn_bk"].reshape(PAIRS, P).T,
        "bv": a["attn_bv"].reshape(PAIRS, P).T,
        "wo": a["attn_wo"].reshape(2 * D, P),
        "bo": a["attn_bo"].reshape(P, 1),
        "proj_w": a["attn_proj_w"],
        "proj_b": a["attn_proj_b"],
        "pos": a["xattn_position_bias"],
        "lnw": a["xattn_ln_weight"],
        "xq": heads(a["xattn_w_q"]), "xk": heads(a["xattn_w_k"]), "xv": xv,
        "xo": a["xattn_w_out"].T.reshape(XH, P, D),
        "aw": _np.concatenate([a["ffn_A"].reshape(E * R, D).T, a["ffn_Wr"].T], axis=1),
        "bw": a["ffn_B"].transpose(0, 2, 1).reshape(E * R, D),
        "br": a["ffn_br"],
    }
    nc = _bacc.Bacc("TRN2", target_bir_lowering=False, num_devices=1)
    arrays, args = {}, []
    for name, v in layout.items():
        v = _np.ascontiguousarray(v)
        arrays[f"in_{name}"] = v
        args.append(nc.dram_tensor(f"in_{name}", v.shape, _mybir.dt.from_np(v.dtype), kind="ExternalInput").ap())
    args.append(nc.dram_tensor("out_x", (B, P, D), _mybir.dt.float32, kind="ExternalOutput").ap())
    decoder_layer(nc, *args)
    r = _run(nc, [arrays], core_ids=[0])
    return r.results[0]["out_x"]
```

```python
from contextlib import ExitStack

import concourse.bass as bass
from concourse import mybir

F32 = mybir.dt.float32
F32R = mybir.dt.float32r
BF16 = mybir.dt.bfloat16
I32 = mybir.dt.int32
U8 = mybir.dt.uint8
ALU = mybir.AluOpType
ACT = mybir.ActivationFunctionType
AX_X = mybir.AxisListType.X

P = 128
B = 8
D = 512
KT = D // P
TOK = B * P
HALF = TOK // 2
HB = B // 2
PAIRS = 8
ITEMS = 2 * PAIRS
XH = 32
GROUP = 4
GROUPS = XH // GROUP
E = 8
R = 16
PROJ_I = 10
PAD = P + 2
CONV = 3
CC = 3 * P
EPS = 1e-5
NEG = -1e9
MASKED = -1e30
BIG = 3e38
RING = 4
N_CONV = CONV * KT
WO_AT, PROJ_AT, CTX_AT = 6, 8, 9
G0 = CTX_AT + 2 * KT
PER_GROUP = 4 * GROUP
SLOT = {"v": [0, 1, 2, 3], "q": [4, 6, 9, 12], "k": [5, 7, 10, 13], "o": [8, 11, 14, 15]}
ORDER = sorted((i, m, h) for m, s in SLOT.items() for h, i in enumerate(s))


def decoder_layer(nc, x, ctx_t, mask, conv_w, conv_b, wq, wk, wv, bq, bk, bv, wo, bo, proj_w, proj_b,
                  pos, lnw, xq, xk, xv, xo, aw, bw, br, out):
    with ExitStack() as ctx:
        def sb(name, shape, dt=F32):
            return ctx.enter_context(nc.sbuf_tensor(name, shape, dt))

        def sem(name):
            return ctx.enter_context(nc.semaphore(name))

        r_a = sb("r_a", [P, 8192], F32R)
        r_x = sb("r_x", [P, 2 * KT * B * PAD], F32R)
        r_c = sb("r_c", [P, 2 * N_CONV * CC], F32R)
        r_q = sb("r_q", [P, 8192], F32R)
        r_o = sb("r_o", [P, 2, HALF], F32R)
        wqkv_r = r_a[:, 0:6144].rearrange("p (s m c) -> p s m c", s=2, m=3)
        wo_r = r_a[:, 6144:8192].rearrange("p (s c) -> p s c", s=2)
        xpad_r = r_x[:, :].rearrange("p (s k b t) -> p s k b t", s=2, k=KT, b=B)
        conv_r = r_c[:, :].rearrange("p (s j c) -> p s j c", s=2, j=N_CONV)
        proj_r = r_c[:, 8192:9216].rearrange("p (s c) -> p s c", s=2)
        qkv_r = r_q[:, 0:6144].rearrange("p (s m t) -> p s m t", s=2, m=3)
        ot_r = r_q[:, 6144:8192].rearrange("p (u s t) -> p u s t", u=2, s=2)
        yt_r = r_x[:, 0:2 * TOK].rearrange("p (s t) -> p s t", s=2)
        xt_r = r_x[:, 0:2 * KT * TOK].rearrange("p (s k t) -> p s k t", s=2, k=KT)
        ct_r = r_c[:, 0:8192].rearrange("p (s k t) -> p s k t", s=2, k=KT)
        w_r = {"q": r_a[:, 0:4096], "k": r_a[:, 4096:8192], "v": r_q[:, 0:4096], "o": r_q[:, 4096:8192]}
        w_r = {m: t.rearrange("p (s h c) -> p s h c", s=2, h=GROUP) for m, t in w_r.items()}

        acc = sb("acc", [P, B, D])
        vals = sb("vals", [P, 2, HB, D])
        va = vals[:, :, :, :].rearrange("p u b c -> p (u b c)").rearrange("p (b c) -> p b c", b=HB)
        qt = sb("qt", [P, HALF])
        kt_ = sb("kt", [P, HALF])
        sc = sb("sc", [P, 2, 2, HB, P])
        scb = sc[:, 0, 0, :, :]
        pt = sb("pt", [P, 2, HALF])
        hb = [sc[:, 0, 1, :, :].rearrange("p b k -> p (b k)"), sc[:, 1, 0, :, :].rearrange("p b k -> p (b k)"),
              sc[:, 1, 1, :, :].rearrange("p b k -> p (b k)"), pt[:, 1, :]]
        bm = sb("bm", [P, 2, HB, P])
        bmrow = bm[:, :, :, :].rearrange("p u b k -> p u (b k)")
        projb_b, lnw_b = bmrow[:, 0, :], bmrow[:, 1, :]
        maskb = sb("maskb", [P, B, P], BF16)
        mask_u = sb("mask_u", [P, B, P], U8)
        anyv = sb("anyv", [P, B])
        pb = sb("pb", [P, GROUP, P])
        ring = sb("ring", [P, RING, D])
        ident = sb("ident", [P, P])
        causal = sb("causal", [P, P])
        cb = sb("cb", [P, 3])
        bqs, bks, bvs, bos = sb("bqs", [P, PAIRS]), sb("bks", [P, PAIRS]), sb("bvs", [P, PAIRS]), sb("bos", [P, 1])
        aws = sb("aws", [P, KT, P + E])
        bws = sb("bws", [P, D])
        brs = sb("brs", [P, E])
        st = sb("st", [P, B, 6])
        mv = sb("mv", [P, B, 2])
        ve = sb("ve", [P, B])
        rs = sb("rs", [P, B])
        nt = sb("nt", [P, B])
        msq = sb("msq", [P, B])
        nmx = sb("nmx", [P, 2, 8])
        sums = sb("sums", [P, 2, 8])
        rinv = sb("rinv", [P, 8])
        scratch = sb("scratch", [P, 1])
        lg = sb("lg", [P, HB, E])
        lmx = sb("lmx", [P, HB])
        lsum = sb("lsum", [P, HB])
        lr = sb("lr", [P, HB])
        scw = sb("scw", [P, HB, E])

        bank = [ctx.enter_context(nc.psum_tensor(f"bank{i}", [P, 512], F32)) for i in range(8)]
        S2, T2, PVB, J0, J1, Y = bank[0:2], bank[2:4], bank[4], bank[5], bank[6], bank[7]
        OB, SX, TX = bank[0:4], bank[4], bank[7]
        CB = [bank[2], bank[3], bank[4], bank[0], bank[1], bank[7]]
        LOW, ROUTE, GT, FB = [J0, bank[2]], [J1, bank[3]], [bank[4], bank[0]], [J0, J1, bank[7], bank[4]]
        TURN = [J0, J1] * 2 + [bank[0], bank[1]] * 2
        PJ = [J0, J1, J0, J1, bank[2], bank[3], bank[4], bank[7]]

        x_ld = [sem(f"x_ld{n}") for n in range(2)]
        cst_ld, mask_ld, lnw_ld = sem("cst_ld"), sem("mask_ld"), sem("lnw_ld")
        w_ld = [sem(f"w_ld{i}") for i in range(RING)]
        pb_ld = [sem(f"pb_ld{h}") for h in range(GROUP)]
        w_hi, w_lo = sem("w_hi"), sem("w_lo")
        tap_ld = [sem(f"tap_ld{t}") for t in range(CONV)]
        tap_hi, tap_lo = sem("tap_hi"), sem("tap_lo")
        id_rdy, cz_rdy, pads_rdy, projb_add, mask_rdy, any_rdy = (
            sem("id_rdy"), sem("cz_rdy"), sem("pads_rdy"), sem("projb_add"), sem("mask_rdy"), sem("any_rdy"))
        xn_rdy, tp_mm, xt_hi, xt_lo, h_rdy, sq_rdy = (
            sem("xn_rdy"), sem("tp_mm"), sem("xt_hi"), sem("xt_lo"), sem("h_rdy"), sem("sq_rdy"))
        cv_mm, cv_hi, cv_lo = sem("cv_mm"), sem("cv_hi"), sem("cv_lo")
        qh_mm, kh_mm, qh_sb, kh_sb = sem("qh_mm"), sem("kh_mm"), sem("qh_sb"), sem("kh_sb")
        va_mm, va_even, va_odd = sem("va_mm"), sem("va_even"), sem("va_odd")
        s_mm, s_max, s_exp, s_rcp, s_norm = sem("s_mm"), sem("s_max"), sem("s_exp"), sem("s_rcp"), sem("s_norm")
        t_mm, pt_even, pt_odd, pv_mm, o_hi, o_lo, wo_mm, y_hi, y_lo, pj_mm, pj_add = (
            sem("t_mm"), sem("pt_even"), sem("pt_odd"), sem("pv_mm"), sem("o_hi"), sem("o_lo"), sem("wo_mm"),
            sem("y_hi"), sem("y_lo"), sem("pj_mm"), sem("pj_add"))
        xv_mm, xv_sb, xq_mm, xq_sb, xk_mm, xk_sb = (
            sem("xv_mm"), sem("xv_sb"), sem("xq_mm"), sem("xq_sb"), sem("xk_mm"), sem("xk_sb"))
        xs_mm, xs_max, xs_exp, xs_rcp, xs_norm, bm_rdy = (
            sem("xs_mm"), sem("xs_max"), sem("xs_exp"), sem("xs_rcp"), sem("xs_norm"), sem("bm_rdy"))
        xt_mm, xp_sb, xpv_mm, xo_hi, xo_lo, xo_mm, xo_add = (
            sem("xt_mm"), sem("xp_sb"), sem("xpv_mm"), sem("xo_hi"), sem("xo_lo"), sem("xo_mm"), sem("xo_add"))
        ad_mm, lg_rdy, lg_exp, g_rdy, gt_mm, gt_sb, f_mm, f_add, out_st = (
            sem("ad_mm"), sem("lg_rdy"), sem("lg_exp"), sem("g_rdy"), sem("gt_mm"), sem("gt_sb"), sem("f_mm"),
            sem("f_add"), sem("out_st"))
        dve_seq = sem("dve_seq")

        cw_v = conv_w.rearrange("t (k p) c -> p t k c", p=P)
        tap_raw = [sc[:, :, :, :, :].rearrange("p u e b k -> p (u e b k)")[:, 0:KT * CC],
                   va[:, :, :].rearrange("p b c -> p (b c)")[:, 0:KT * CC],
                   va[:, :, :].rearrange("p b c -> p (b c)")[:, KT * CC:2 * KT * CC]]
        tap_r = r_c[:, :].rearrange("p (s t c) -> p s t c", s=2, t=CONV)
        staged = []
        for m, w in enumerate((wq, wk, wv)):
            for s in range(2):
                c = slice(s * D, s * D + D)
                staged.append((w[:, c], wqkv_r[:, 0, m, c], wqkv_r[:, 1, m, c], D))
        wo_v = wo.rearrange("(j p) c -> p j c", p=P)
        for s in range(2):
            c = slice(s * D, s * D + D)
            staged.append((wo_v[:, 4 * s:4 * s + 4, :], wo_r[:, 0, c], wo_r[:, 1, c], D))
        staged.append((proj_w, proj_r[:, 0, :], proj_r[:, 1, :], D))
        for k in range(KT):
            for n in range(2):
                c = slice(n * HALF, n * HALF + HALF)
                staged.append((ctx_t[k * P:(k + 1) * P, c], ct_r[:, 0, k, c], ct_r[:, 1, k, c], HALF))
        assert len(staged) == G0
        xw = {"q": xq, "k": xk, "v": xv, "o": xo}

        def slot_of(pos):
            return pos % RING

        def group_item(j):
            _, m, h = ORDER[j]
            return m, h, w_r[m][:, 0, h, :], w_r[m][:, 1, h, :]

        def pos_v(first, h):
            return pos[bass.ds(first + h, 1), :, :].rearrange("a q k -> (a q) k")

        block = ctx.enter_context(nc.Block())

        @block.sync
        def _(sp):
            def load_static(pos, src, cols):
                if pos >= RING:
                    sp.wait_ge(w_lo, pos - RING + 1)
                dst = ring[:, slot_of(pos), 0:cols]
                if len(src.shape) == 3:
                    dst = dst.rearrange("p (j c) -> p j c", j=src.shape[1])
                sp.dma_start(dst, src).then_inc(w_ld[slot_of(pos)], 16)

            xv_ = x.rearrange("b t d -> t b d")
            sp.dma_start(acc[:, 0:HB, :], xv_[:, 0:HB, :]).then_inc(x_ld[0], 16)
            for t in range(CONV):
                sp.dma_start(tap_raw[t].rearrange("p (k c) -> p k c", k=KT), cw_v[:, t, :, :]).then_inc(tap_ld[t], 16)
            sp.dma_start(acc[:, HB:B, :], xv_[:, HB:B, :]).then_inc(x_ld[1], 16)
            for pos, (src, _, _, cols) in enumerate(staged):
                load_static(pos, src, cols)
            for h in range(GROUP):
                sp.dma_start(pb[:, h, :], pos_v(0, h)).then_inc(pb_ld[h], 16)
            for j in range(PER_GROUP):
                m, h, _, _ = group_item(j)
                load_static(G0 + j, xw[m][h], D)

            with sp.Fori(0, GROUPS - 1) as g:
                for j in range(PER_GROUP):
                    m, h, _, _ = group_item(j)
                    if m == "q":
                        sp.wait_ge(bm_rdy, 8 * g + 4 + h + 1)
                        sp.dma_start(pb[:, h, :], pos_v((g + 1) * GROUP, h)).then_inc(pb_ld[h], 16)
                    pos = G0 + PER_GROUP + j
                    sp.wait_ge(w_lo, PER_GROUP * g + pos - RING + 1)
                    src = xw[m][bass.ds((g + 1) * GROUP + h, 1), :, :].rearrange("a p c -> (a p) c")
                    sp.dma_start(ring[:, slot_of(pos), :], src).then_inc(w_ld[slot_of(pos)], 16)

            for b in range(B):
                sp.wait_ge(f_add, b + 1)
                sp.dma_start(out[b], acc[:, b, :]).then_inc(out_st, 16)
            sp.wait_ge(out_st, 16 * B)

        @block.gpsimd
        def _(pool):
            def split_hi(pos, dst, cols):
                pool.wait_ge(w_ld[slot_of(pos)], 16 * (pos // RING + 1))
                nc.gpsimd.tensor_copy(dst, ring[:, slot_of(pos), 0:cols]).then_inc(w_hi, 1)

            nc.gpsimd.memset(ident[:], 0.0).then_inc(cz_rdy, 1)
            nc.gpsimd.memset(causal[:], 0.0).then_inc(cz_rdy, 1)
            nc.gpsimd.memset(xpad_r[:, :, :, :, 0:PAD:PAD - 1].bitcast(F32)
                             .rearrange("p s k b t -> p (s k b) t"), 0.0).then_inc(pads_rdy, 1)
            pool.wait_ge(cz_rdy, 2)
            nc.gpsimd.affine_select(out=ident[:], in_=ident[:], compare_op=ALU.not_equal, fill=1.0, base=0,
                                    pattern=[[-1, P]], channel_multiplier=1).then_inc(id_rdy, 1)
            nc.gpsimd.affine_select(out=causal[:], in_=causal[:], compare_op=ALU.is_ge, fill=NEG, base=0,
                                    pattern=[[-1, P]], channel_multiplier=1).then_inc(id_rdy, 1)
            for p_ in range(WO_AT + 2):
                _, hi, _, cols = staged[p_]
                split_hi(p_, hi, cols)
            pool.wait_ge(cst_ld, 16 * N_CST)
            pool.wait_ge(xn_rdy, B)
            for b in range(B):
                nc.gpsimd.tensor_tensor(acc[:, b, :], acc[:, b, :], projb_b, ALU.add).then_inc(projb_add, 1)
            pool.wait_ge(cv_mm, 6)
            for p_ in range(PROJ_AT, G0):
                _, hi, _, cols = staged[p_]
                split_hi(p_, hi, cols)
            pool.wait_ge(mask_ld, 16)
            nc.gpsimd.tensor_scalar(maskb[:, :, :], mask_u[:, :, :], 1.0, -MASKED, ALU.subtract, ALU.mult)\
                .then_inc(mask_rdy, 1)

            def bias_mask(c, q):
                h, n = q % GROUP, q // GROUP % 2
                pool.wait_ge(pb_ld[h], 16 * c[1] + 16)
                nc.gpsimd.tensor_tensor(bm[:, q % 2, :, :], maskb[:, HB * n:HB * n + HB, :],
                                        pb[:, h, :].unsqueeze(1).broadcast_to((P, HB, P)), ALU.add)\
                    .then_inc(bm_rdy, 1)

            pool.wait_ge(mask_rdy, 1)
            pool.wait_ge(projb_add, B)
            bias_mask((0, 0), 0)
            for b in range(B):
                pool.wait_ge(h_rdy, b + 1)
                nc.gpsimd.tensor_tensor(acc[:, b, :], acc[:, b, :], hb[b % HB], ALU.add).then_inc(xo_add, 1)
            pool.wait_ge(xn_rdy, 2 * B)
            bias_mask((1, 0), 1)

            def group(g, last):
                for q in range(1, 9):
                    c = 8 * g + q
                    if not last or q < 7:
                        pool.wait_ge(xs_max, 4 * c)
                        bias_mask((c + 1, g + (q + 1) // 8), (q + 1) % 8)

            with pool.Fori(0, GROUPS - 1) as g:
                group(g, False)
            group(GROUPS - 1, True)

        @block.scalar
        def _(act):
            def split_hi(pos):
                act.wait_ge(w_ld[slot_of(pos)], 16 * (pos // RING + 1))
                nc.scalar.activation(group_item(pos - G0)[2], ring[:, slot_of(pos), :], ACT.Copy).then_inc(w_hi, 1)

            def tile_hi(b):
                act.wait_ge(tp_mm, b + 1)
                nc.scalar.activation(xpad_r[:, 0, :, b, 1:1 + P],
                                     bank[b % 2][:, :].rearrange("p (k t) -> p k t", k=KT), ACT.Copy)\
                    .then_inc(xt_hi, 1)

            for t in range(CONV):
                act.wait_ge(tap_ld[t], 16)
                nc.scalar.activation(tap_r[:, 0, t, :], tap_raw[t], ACT.Copy).then_inc(tap_hi, 1)
            for b in range(HB):
                tile_hi(b)
            small = [(cb[:], conv_b), (bqs[:], bq), (bks[:], bk), (bvs[:], bv), (bos[:], bo),
                     (projb_b, proj_b.partition_broadcast(P)), (aws[:, :, :], aw.rearrange("(k p) c -> p k c", p=P)),
                     (bws[:], bw), (brs[:], br.partition_broadcast(P))]
            assert len(small) == N_CST
            for dst, src in small:
                act.dma_start(dst, src).then_inc(cst_ld, 16)
            act.dma_start(lnw_b, lnw.partition_broadcast(P)).then_inc(lnw_ld, 16)
            act.dma_start(mask_u[:, :, :], mask.rearrange("b q k -> q b k")).then_inc(mask_ld, 16)

            def conv_hi(j):
                n, m = divmod(j, 3)
                act.wait_ge(cv_mm, j + 1)
                nc.scalar.activation(qkv_r[:, 0, m, n * HALF:(n + 1) * HALF], CB[j][:, :], ACT.Identity,
                                     bias=cb[:, m:m + 1]).then_inc(cv_hi, 1)

            act.wait_ge(cst_ld, 16 * N_CST)
            conv_hi(0)
            tile_hi(4)
            tile_hi(5)
            conv_hi(1)
            tile_hi(6)
            tile_hi(7)
            for j in range(2, 5):
                conv_hi(j)

            def kh_out(i):
                act.wait_ge(kh_mm, i + 1)
                nc.scalar.activation(kt_[:], J1[:, :], ACT.Identity, bias=bks[:, i % PAIRS:i % PAIRS + 1])\
                    .then_inc(kh_sb, 1)

            kh_out(0)
            conv_hi(5)
            for i in range(ITEMS + 2):
                for e in range(2):
                    if e == 1 and i + 1 < ITEMS:
                        kh_out(i + 1)
                    if i < ITEMS:
                        for b in range(HB):
                            k = 4 * e + b
                            act.wait_ge(s_max, 8 * i + k + 1)
                            t = sc[:, i % 2, e, b, :]
                            nc.scalar.activation(t, t, ACT.Exp, scale=-1.0, bias=nmx[:, i % 2, k:k + 1],
                                                 accum_out=sums[:, i % 2, k:k + 1]).then_inc(s_exp, 1)
                    if e == 0 and 1 <= i <= ITEMS:
                        act.wait_ge(t_mm, i)
                        nc.scalar.copy(pt[:, 0, :], T2[0][:, :]).then_inc(pt_even, 1)
                if i - 2 in (PAIRS - 1, ITEMS - 1):
                    n = (i - 2) // PAIRS
                    act.wait_ge(wo_mm, i - 1)
                    nc.scalar.activation(yt_r[:, 0, n * HALF:(n + 1) * HALF], Y[:, :], ACT.Identity,
                                         bias=bos[:, 0:1]).then_inc(y_hi, 1)
                if i == ITEMS:
                    act.wait_ge(xv_mm, 1)
                    nc.scalar.copy(vals[:, 0, 0, :], J0[:, :]).then_inc(xv_sb, 1)
                if 1 <= i <= ITEMS:
                    act.wait_ge(pv_mm, i)
                    p_ = (i - 1) % PAIRS
                    nc.scalar.activation(ot_r[:, (i - 1) % 2, 0, :], PVB[:, :], ACT.Identity,
                                         bias=bvs[:, p_:p_ + 1]).then_inc(o_hi, 1)
                if i % PAIRS == 0 and i < ITEMS:
                    for m in range(0, B, 2):
                        act.wait_ge(va_mm, i + m + 1)
                        nc.scalar.copy(va[:, m // 2, 0:D], J0[:, :]).then_inc(va_even, 1)
                if i == ITEMS - 1:
                    act.wait_ge(kh_mm, ITEMS)
                    for s in range(GROUP):
                        split_hi(G0 + s)

            def value(b):
                act.wait_ge(xv_mm, b + 1)
                nc.scalar.copy(vals[:, 0, b, :], (J0, J1)[b % 2][:, :]).then_inc(xv_sb, 1)

            def square(b):
                act.wait_ge(h_rdy, b + 1)
                nc.scalar.activation(xt_r[:, 0, :, b * P:(b + 1) * P],
                                     hb[b % HB].rearrange("p (k t) -> p k t", k=KT), ACT.Square,
                                     accum_out=msq[:, b:b + 1]).then_inc(sq_rdy, 1)

            def xtile_hi(b):
                act.wait_ge(tp_mm, B + b + 1)
                nc.scalar.activation(xt_r[:, 0, :, b * P:(b + 1) * P],
                                     bank[b % 2][:, :].rearrange("p (k t) -> p k t", k=KT), ACT.Copy)\
                    .then_inc(xt_hi, 1)

            def first_quarters_split(a, z):
                act.wait_ge(wo_mm, ITEMS)
                for j in range(a, z):
                    split_hi(G0 + j)

            value(1)
            for b in range(HB):
                square(b)
            value(2)
            value(3)
            first_quarters_split(4, 6)
            for b in range(HB):
                xtile_hi(b)
            for b in range(HB, B):
                square(b)

            def quarter(c, q, back, front):
                if front:
                    act.wait_ge(xq_mm, c + 1)
                    nc.scalar.copy(qt[:], J0[:, :]).then_inc(xq_sb, 1)
                if back:
                    act.wait_ge(xt_mm, c)
                    nc.scalar.copy(pt[:, 0, :], TX[:, :]).then_inc(xp_sb, 1)
                if front:
                    act.wait_ge(xk_mm, c + 1)
                    nc.scalar.copy(kt_[:], J1[:, :]).then_inc(xk_sb, 1)
                if back:
                    act.wait_ge(xpv_mm, c)
                    nc.scalar.activation(r_o[:, 0, :], TX[:, :], ACT.Copy).then_inc(xo_hi, 1)
                if front:
                    for b in range(HB):
                        act.wait_ge(xs_max, 4 * c + b + 1)
                        t = scb[:, b, :]
                        nc.scalar.activation(t, t, ACT.Exp, scale=-1.0, bias=nmx[:, 0, b:b + 1],
                                             accum_out=sums[:, 0, b:b + 1]).then_inc(xs_exp, 1)
                    if front != "last":
                        act.wait_ge(xv_mm, c + 5)
                        u = (q // GROUP + 1) % 2
                        nc.scalar.copy(vals[:, u, q % GROUP, :], J0[:, :]).then_inc(xv_sb, 1)

            quarter(0, 0, False, True)
            first_quarters_split(6, 9)
            for b in range(HB, B):
                xtile_hi(b)
            first_quarters_split(9, PER_GROUP)
            with act.Fori(0, GROUPS - 1) as g:
                for q in range(1, 9):
                    quarter(8 * g + q, q, True, True)
            def atile(b):
                act.wait_ge(tp_mm, 2 * B + b + 1)
                nc.scalar.copy(vals[:, 0, b % HB, :], TURN[b][:, :]).then_inc(xt_hi, 1)

            def gates(n):
                act.wait_ge(lg_rdy, n + 1)
                nc.scalar.activation(lg[:, :, :], lg[:, :, :], ACT.Exp).then_inc(lg_exp, 1)

            def turned(n):
                act.wait_ge(gt_mm, n + 1)
                if n:
                    act.wait_ge(f_mm, HB)
                nc.scalar.copy(kt_[:], GT[n][:, :]).then_inc(gt_sb, 1)

            for q in range(1, 9):
                quarter(8 * (GROUPS - 1) + q, q, True, False if q == 8 else "last" if q >= 4 else True)
                if q in (6, 7):
                    atile(2 * q - 12)
                    atile(2 * q - 11)
            gates(0)
            turned(0)
            for b in range(HB, B):
                atile(b)
            gates(1)
            turned(1)

        @block.vector
        def _(dve):
            done = [0]

            def link(ins):
                done[0] += 1
                ins.then_inc(dve_seq, 1)
                dve.wait_ge(dve_seq, done[0])

            def split_lo(pos, base, hi, lo, cols):
                dve.wait_ge(w_hi, base + pos + 1)
                nc.vector.tensor_tensor(lo, ring[:, slot_of(pos), 0:cols], hi.bitcast(F32), ALU.subtract)\
                    .then_inc(w_lo, 1)

            def split_static(a, z):
                for p_ in range(a, z):
                    if p_ < G0:
                        _, hi, lo, cols = staged[p_]
                        split_lo(p_, 0, hi, lo, cols)
                    else:
                        _, _, hi, lo = group_item(p_ - G0)
                        split_lo(p_, 0, hi, lo, D)

            def rsqrt(cols):
                v, r, t = ve[:, cols], rs[:, cols], nt[:, cols]
                link(nc.vector.tensor_scalar(r.bitcast(I32), v.bitcast(I32), 1, None, ALU.logical_shift_right))
                link(nc.vector.tensor_scalar(r.bitcast(I32), r.bitcast(I32), -1.0, float(0x5F3759DF), ALU.mult, ALU.add))
                for _ in range(3):
                    link(nc.vector.tensor_tensor(t, r, r, ALU.mult))
                    link(nc.vector.scalar_tensor_tensor(t, t, -0.5, v, ALU.mult, ALU.mult))
                    link(nc.vector.scalar_tensor_tensor(r, t, 1.5, r, ALU.add, ALU.mult))

            def sums_of(n):
                for b in range(HB * n, HB * n + HB):
                    ins = nc.vector.bn_stats(st[:, b, :], acc[:, b, :])
                return ins

            def moments(n, stats=True):
                if stats:
                    link(sums_of(n))
                for b in range(HB * n, HB * n + HB):
                    ins = nc.vector.bn_aggr(mv[:, b, :], st[:, b, :])
                link(ins)
                cols = slice(HB * n, HB * n + HB)
                link(nc.vector.tensor_scalar(ve[:, cols], mv[:, cols, 1], EPS, None, ALU.add))
                rsqrt(cols)

            def centre(dst, b):
                return nc.vector.tensor_scalar(dst, acc[:, b, :], mv[:, b, 0:1], rs[:, b:b + 1],
                                               ALU.subtract, ALU.mult)

            def tile_lo(k, dst, hi):
                dve.wait_ge(xt_hi, k + 1)
                src = bank[k % 2][:, :].rearrange("p (k t) -> p k t", k=KT)
                nc.vector.tensor_tensor(dst, src, hi.bitcast(F32), ALU.subtract).then_inc(xt_lo, 1)

            def norm_tile(b):
                if b >= 2:
                    dve.wait_ge(tp_mm, b - 1)
                centre(pt[:, b % 2, :], b).then_inc(xn_rdy, 1)

            def norm_lo(b):
                tile_lo(b, xpad_r[:, 1, :, b, 1:1 + P], xpad_r[:, 0, :, b, 1:1 + P])

            def tap_rest(t):
                dve.wait_ge(tap_hi, t + 1)
                nc.vector.tensor_tensor(tap_r[:, 1, t, :], tap_raw[t], tap_r[:, 0, t, :].bitcast(F32), ALU.subtract)\
                    .then_inc(tap_lo, 1)

            def conv_rest(j):
                n, m = divmod(j, 3)
                t = slice(n * HALF, (n + 1) * HALF)
                dve.wait_ge(cv_hi, j + 1)
                nc.vector.scalar_tensor_tensor(qkv_r[:, 1, m, t], CB[j][:, :], cb[:, m:m + 1],
                                               qkv_r[:, 0, m, t].bitcast(F32), ALU.add, ALU.subtract)\
                    .then_inc(cv_lo, 1)

            dve.wait_ge(pads_rdy, 1)
            dve.wait_ge(x_ld[0], 16)
            moments(0)
            norm_tile(0)
            norm_tile(1)
            tap_rest(0)
            for b in range(2, HB + 2):
                norm_lo(b - 2)
                if b < HB:
                    norm_tile(b)
            tap_rest(1)
            tap_rest(2)
            dve.wait_ge(x_ld[1], 16)
            moments(1)
            norm_tile(4)
            norm_tile(5)
            dve.wait_ge(cst_ld, 16 * N_CST)
            conv_rest(0)
            norm_lo(4)
            norm_tile(6)
            norm_lo(5)
            norm_tile(7)
            split_static(0, WO_AT)
            conv_rest(1)
            norm_lo(6)
            norm_lo(7)
            for j in range(2, 5):
                conv_rest(j)
            split_static(WO_AT, WO_AT + 2)

            def qh_out(i):
                dve.wait_ge(qh_mm, i + 1)
                nc.vector.tensor_scalar(qt[:], J0[:, :], bqs[:, i % PAIRS:i % PAIRS + 1], 0.125,
                                        ALU.add, ALU.mult).then_inc(qh_sb, 1)

            def group_rest(a, z):
                split_static(G0 + a, G0 + z)

            def project_add(b):
                dve.wait_ge(pj_mm, b + 1)
                nc.vector.tensor_tensor(acc[:, b, :], acc[:, b, :], PJ[b][:, :], ALU.add).then_inc(pj_add, 1)

            qh_out(0)
            conv_rest(5)
            dve.wait_ge(id_rdy, 2)
            dve.wait_ge(projb_add, B)
            for i in range(ITEMS + 2):
                if i < ITEMS:
                    dve.wait_ge(s_mm, i + 1)
                    for k in range(8):
                        e, b = divmod(k, HB)
                        nc.vector.tensor_tensor_reduce(
                            sc[:, i % 2, e, b, :], S2[e][:, b * P:(b + 1) * P], causal[:], -1.0, BIG,
                            ALU.add, ALU.min, nmx[:, i % 2, k:k + 1]).then_inc(s_max, 1)
                if 1 <= i <= ITEMS:
                    dve.wait_ge(t_mm, i)
                    nc.vector.tensor_copy(pt[:, 1, :], T2[1][:, :]).then_inc(pt_odd, 1)
                if i + 1 < ITEMS:
                    qh_out(i + 1)
                if i < ITEMS:
                    for e in range(2):
                        k = slice(4 * e, 4 * e + 4)
                        dve.wait_ge(s_exp, 8 * i + 4 * e + 4)
                        nc.vector.reciprocal(rinv[:, k], sums[:, i % 2, k]).then_inc(s_rcp, 1)
                        dve.wait_ge(s_rcp, 2 * i + e + 1)
                        t = sc[:, i % 2, e, :, :]
                        nc.vector.tensor_tensor(t, t, rinv[:, k].unsqueeze(2).broadcast_to((P, HB, P)), ALU.mult)\
                            .then_inc(s_norm, 1)
                        if e == 0 and 1 <= i <= G0 - PROJ_AT:
                            split_static(PROJ_AT + i - 1, PROJ_AT + i)
                if i == ITEMS:
                    moments(0, stats=False)
                    for j in range(HB - 1):
                        centre(hb[j], j).then_inc(h_rdy, 1)
                if i - 2 in (PAIRS - 1, ITEMS - 1):
                    n = (i - 2) // PAIRS
                    t = slice(n * HALF, (n + 1) * HALF)
                    dve.wait_ge(y_hi, n + 1)
                    nc.vector.scalar_tensor_tensor(yt_r[:, 1, t], Y[:, :], bos[:, 0:1],
                                                   yt_r[:, 0, t].bitcast(F32), ALU.add, ALU.subtract)\
                        .then_inc(y_lo, 1)
                if 1 <= i <= ITEMS:
                    p_, u = (i - 1) % PAIRS, (i - 1) % 2
                    dve.wait_ge(o_hi, i)
                    nc.vector.scalar_tensor_tensor(ot_r[:, u, 1, :], PVB[:, :], bvs[:, p_:p_ + 1],
                                                   ot_r[:, u, 0, :].bitcast(F32), ALU.add, ALU.subtract)\
                        .then_inc(o_lo, 1)
                if i % PAIRS == 0 and i < ITEMS:
                    for m in range(1, B, 2):
                        dve.wait_ge(va_mm, i + m + 1)
                        nc.vector.tensor_copy(va[:, m // 2, D:2 * D], J1[:, :]).then_inc(va_odd, 1)
                if i in (PROJ_I, PROJ_I + 1):
                    project_add(2 * (i - PROJ_I))
                    project_add(2 * (i - PROJ_I) + 1)
                if i == PROJ_I + 3:
                    dve.wait_ge(pj_add, HB)
                    link(sums_of(0))
                if i == ITEMS - 1:
                    group_rest(0, GROUP)
                if i == ITEMS:
                    centre(hb[3], 3).then_inc(h_rdy, 1)
            for b in range(HB, B):
                project_add(b)
            dve.wait_ge(pj_add, B)

            dve.wait_ge(lnw_ld, 16)

            def scale_rows(n):
                cols = slice(HB * n, HB * n + HB)
                dve.wait_ge(sq_rdy, HB * (n + 1))
                link(nc.vector.tensor_scalar(ve[:, cols], msq[:, cols], 1.0 / D, EPS, ALU.mult, ALU.add))
                rsqrt(cols)
                for j in range(HB):
                    b = HB * n + j
                    dve.wait_ge(xo_add, b + 1)
                    nc.vector.scalar_tensor_tensor(hb[j], hb[j], rs[:, b:b + 1], lnw_b,
                                                   ALU.mult, ALU.mult).then_inc(xn_rdy, 1)

            def xtile_rest(b):
                t = slice(b * P, (b + 1) * P)
                tile_lo(B + b, xt_r[:, 1, :, t], xt_r[:, 0, :, t])

            scale_rows(0)
            for b in range(HB):
                xtile_rest(b)
            group_rest(4, 6)
            moments(1)
            for j in range(HB):
                dve.wait_ge(tp_mm, B + j + 1)
                centre(hb[j], HB + j).then_inc(h_rdy, 1)
            dve.wait_ge(mask_ld, 16)
            nc.vector.tensor_reduce(anyv[:], mask_u[:, :, :], AX_X, ALU.max).then_inc(any_rdy, 1)
            dve.wait_ge(any_rdy, 1)

            def quarter(c, q, back, front):
                if back:
                    dve.wait_ge(xo_hi, c)
                    nc.vector.tensor_tensor(r_o[:, 1, :], TX[:, :], r_o[:, 0, :].bitcast(F32), ALU.subtract)\
                        .then_inc(xo_lo, 1)
                if front:
                    n = q // GROUP % 2
                    dve.wait_ge(xs_mm, c + 1)
                    dve.wait_ge(bm_rdy, c + 1)
                    nc.vector.memset(scratch[:], 0.0)
                    for b in range(HB):
                        nc.vector.tensor_tensor_reduce(
                            scb[:, b, :], SX[:, b * P:(b + 1) * P], bm[:, q % 2, b, :], -1.0, BIG,
                            ALU.add, ALU.min, nmx[:, 0, b:b + 1]).then_inc(xs_max, 1)
                    dve.wait_ge(xs_exp, 4 * c + 4)
                    nc.vector.reciprocal(rinv[:, 0:HB], sums[:, 0, 0:HB]).then_inc(xs_rcp, 1)
                    dve.wait_ge(xs_rcp, 2 * c + 1)
                    nc.vector.tensor_tensor(rinv[:, 0:HB], rinv[:, 0:HB], anyv[:, HB * n:HB * n + HB], ALU.mult)\
                        .then_inc(xs_rcp, 1)
                    dve.wait_ge(xs_rcp, 2 * c + 2)
                    nc.vector.tensor_tensor(scb, scb, rinv[:, 0:HB].unsqueeze(2).broadcast_to((P, HB, P)), ALU.mult)\
                        .then_inc(xs_norm, 1)

            def add_out(c, n):
                dve.wait_ge(xo_mm, c)
                for b in range(HB):
                    a = acc[:, HB * n + b, :]
                    nc.vector.tensor_tensor(a, a, OB[b][:, :], ALU.add).then_inc(xo_add, 1)

            quarter(0, 0, False, True)
            group_rest(6, 9)
            scale_rows(1)
            for b in range(HB, B):
                xtile_rest(b)
            group_rest(9, PER_GROUP)
            with dve.Fori(0, GROUPS - 1) as g:
                base = PER_GROUP * g

                def split(m, s):
                    j = SLOT[m][s]
                    pos = G0 + PER_GROUP + j
                    _, _, hi, low = group_item(j)
                    dve.wait_ge(w_ld[slot_of(pos)], 16 * (pos // RING + 1) + PER_GROUP // RING * 16 * g)
                    nc.vector.tensor_copy(hi, ring[:, slot_of(pos), :]).then_inc(w_hi, 1)
                    split_lo(pos, base, hi, low, D)

                for q in range(1, 9):
                    c = 8 * g + q
                    h = q - GROUP
                    if q == 4:
                        dve.wait_ge(xv_mm, c + 4)
                        for s in range(GROUP):
                            split("v", s)
                    quarter(c, q, True, True)
                    if 4 <= q < 8:
                        dve.wait_ge(xk_mm, c + 1)
                        split("q", h)
                        split("k", h)
                    if q % GROUP == 0:
                        add_out(c, q // GROUP - 1)
                    if 5 <= q:
                        dve.wait_ge(xo_mm, c)
                        split("o", h - 1)
            def centre_half(n):
                moments(n)
                for j in range(HB):
                    b = HB * n + j
                    if n:
                        dve.wait_ge(tp_mm, 2 * B + j + 1)
                    centre(hb[j], b).then_inc(xn_rdy, 1)

            def route(n):
                dve.wait_ge(ad_mm, n + 1)
                link(nc.vector.tensor_tensor(lg[:, :, :], ROUTE[n][:, 0:HB * E].rearrange("p (b e) -> p b e", b=HB),
                                             brs[:].unsqueeze(1).broadcast_to((P, HB, E)), ALU.add))
                link(nc.vector.tensor_reduce(lmx[:], lg[:, :, :], AX_X, ALU.max))
                nc.vector.tensor_tensor(lg[:, :, :], lg[:, :, :], lmx[:].unsqueeze(2).broadcast_to((P, HB, E)),
                                        ALU.subtract).then_inc(lg_rdy, 1)
                dve.wait_ge(lg_exp, n + 1)
                link(nc.vector.tensor_reduce(lsum[:], lg[:, :, :], AX_X, ALU.add))
                link(nc.vector.reciprocal(lr[:], lsum[:]))
                link(nc.vector.tensor_scalar(lr[:], lr[:], 2.0 * E, None, ALU.mult))
                link(nc.vector.tensor_tensor(scw[:, :, :], lg[:, :, :], lr[:].unsqueeze(2).broadcast_to((P, HB, E)),
                                             ALU.mult))
                gates = scw[:, :, :].rearrange("p b e -> p (b e)").unsqueeze(2).broadcast_to((P, HB * E, R))
                nc.vector.tensor_tensor(bmrow[:, n, :].rearrange("p (m r) -> p m r", r=R),
                                        LOW[n][:, :].rearrange("p (m r) -> p m r", r=R), gates, ALU.mult)\
                    .then_inc(g_rdy, 1)

            def finish(b):
                dve.wait_ge(f_mm, b + 1)
                nc.vector.tensor_tensor(acc[:, b, :], acc[:, b, :], FB[b % HB][:, :], ALU.add).then_inc(f_add, 1)

            for q in range(1, 9):
                c = 8 * (GROUPS - 1) + q
                quarter(c, q, True, q < 8)
                if q == 8:
                    route(0)
                if q % GROUP == 0:
                    add_out(c, q // GROUP - 1)
                if q == 5:
                    dve.wait_ge(xo_add, B * GROUPS + HB)
                    centre_half(0)
            dve.wait_ge(xo_add, B + B * GROUPS)
            centre_half(1)
            for b in range(HB):
                finish(b)
            route(1)
            for b in range(HB, B):
                finish(b)

        @block.tensor
        def _(pe):
            def three(dst, a, w, first=True, last=True):
                nc.tensor.matmul(dst, a(0), w(0), start=first, stop=False)
                nc.tensor.matmul(dst, a(1), w(0), start=False, stop=False)
                return nc.tensor.matmul(dst, a(0), w(1), start=False, stop=last)

            def tile_turn(k, src, dst):
                pe.wait_ge(xn_rdy, k + 1)
                for kt in range(KT):
                    ins = nc.tensor.transpose(dst[:, kt * P:(kt + 1) * P], src[:, kt * P:(kt + 1) * P], ident[:])
                ins.then_inc(tp_mm, 1)

            def first_turn(b):
                if b >= 2:
                    pe.wait_ge(xt_lo, b - 1)
                tile_turn(b, pt[:, b % 2, :], bank[b % 2])

            def conv(n, m, j):
                t, kt = divmod(j, KT)
                ins = three(CB[3 * n + m][:, :].rearrange("p (b t) -> p b t", b=HB),
                            lambda s: conv_r[:, s, j, m * P:(m + 1) * P],
                            lambda s: xpad_r[:, s, kt, HB * n:HB * n + HB, t:t + P],
                            j == 0, j == N_CONV - 1)
                if j == N_CONV - 1:
                    ins.then_inc(cv_mm, 1)

            pe.wait_ge(id_rdy, 2)
            for b in range(HB):
                first_turn(b)
            pe.wait_ge(xt_lo, HB)
            for m in range(3):
                for j in range(N_CONV):
                    if m == 0 and j % KT == 0:
                        pe.wait_ge(tap_lo, j // KT + 1)
                    if m and j % 6 == 3:
                        first_turn(2 * m + 2 + j // 6)
                    conv(0, m, j)
            pe.wait_ge(xt_lo, B)
            for m in range(2):
                for j in range(N_CONV):
                    conv(1, m, j)

            def xvalues(dst, b):
                for kt in range(KT):
                    ins = three(dst, lambda s: ct_r[:, s, kt, b * P:(b + 1) * P],
                                lambda s: w_r["v"][:, s, kt, :], kt == 0, kt == KT - 1)
                ins.then_inc(xv_mm, 1)

            def project(b):
                three(PJ[b][:, :], lambda s: yt_r[:, s, b * P:(b + 1) * P], lambda s: proj_r[:, s, :])\
                    .then_inc(pj_mm, 1)

            def head_proj(i, m, dst, done):
                n, p_ = divmod(i, PAIRS)
                three(dst, lambda s: wqkv_r[:, s, m, p_ * P:(p_ + 1) * P],
                      lambda s: qkv_r[:, s, m, n * HALF:(n + 1) * HALF]).then_inc(done, 1)

            pe.wait_ge(cv_lo, 2)
            pe.wait_ge(w_lo, WO_AT)
            head_proj(0, 0, J0[:, :], qh_mm)
            head_proj(0, 1, J1[:, :], kh_mm)
            for j in range(N_CONV):
                conv(1, 2, j)
            pe.wait_ge(cv_lo, 5)
            for i in range(ITEMS + 2):
                if i < ITEMS:
                    pe.wait_ge(qh_sb, i + 1)
                    pe.wait_ge(kh_sb, i + 1)
                    if i:
                        pe.wait_ge(s_max, 8 * i)
                    for b in range(HB):
                        for e in range(2):
                            t, h = slice(b * P, (b + 1) * P), slice(64 * e, 64 * e + 64)
                            ins = nc.tensor.matmul(S2[e][:, t], qt[h, t], kt_[h, t], start=True, stop=True)
                    ins.then_inc(s_mm, 1)
                if 1 <= i <= ITEMS:
                    for e in range(2):
                        pe.wait_ge(s_norm, 2 * i - 1 + e)
                        for b in range(HB):
                            ins = nc.tensor.transpose(T2[e][:, b * P:(b + 1) * P], sc[:, (i - 1) % 2, e, b, :], ident[:])
                    ins.then_inc(t_mm, 1)
                if i + 1 < ITEMS:
                    if i in (PROJ_I + 1, PROJ_I + 2):
                        pe.wait_ge(pj_add, 2 * (i - PROJ_I))
                    if i == 1:
                        pe.wait_ge(cv_lo, 6)
                    if i >= 1:
                        pe.wait_ge(va_even, HB * ((i - 1) // PAIRS + 1))
                        pe.wait_ge(va_odd, HB * ((i - 1) // PAIRS + 1))
                    head_proj(i + 1, 0, J0[:, :], qh_mm)
                    head_proj(i + 1, 1, J1[:, :], kh_mm)
                if i >= 2:
                    p_, u = (i - 2) % PAIRS, i % 2
                    pe.wait_ge(o_lo, i - 1)
                    if i == 2:
                        pe.wait_ge(w_lo, WO_AT + 2)
                    if i - 2 == PAIRS:
                        pe.wait_ge(y_lo, 1)
                    three(Y[:, :], lambda s: wo_r[:, s, p_ * P:(p_ + 1) * P], lambda s: ot_r[:, u, s, :],
                          p_ == 0, p_ == PAIRS - 1).then_inc(wo_mm, 1)
                if i == ITEMS:
                    pe.wait_ge(w_lo, G0 + GROUP)
                    xvalues(J0[:, :], 0)
                if 1 <= i <= ITEMS:
                    p_ = (i - 1) % PAIRS
                    pe.wait_ge(pt_even, i)
                    pe.wait_ge(pt_odd, i)
                    for b in range(HB):
                        for e in range(2):
                            ins = nc.tensor.matmul(PVB[64 * e:64 * e + 64, b * P:(b + 1) * P],
                                                   va[:, b, p_ * P + 64 * e:p_ * P + 64 * e + 64],
                                                   pt[:, e, b * P:(b + 1) * P], start=True, stop=True)
                    ins.then_inc(pv_mm, 1)
                if i % PAIRS == 0 and i < ITEMS:
                    n = i // PAIRS
                    for m in range(B):
                        if m < 2:
                            pe.wait_ge((qh_sb, kh_sb)[m], i + 2)
                        else:
                            pe.wait_ge((va_even, va_odd)[m % 2], HB * n + m // 2)
                        b = HB * n + m // 2
                        three((J0, J1)[m % 2][:, :], lambda s: qkv_r[:, s, 2, b * P:(b + 1) * P],
                              lambda s: wqkv_r[:, s, 2, m % 2 * D:(m % 2 + 1) * D]).then_inc(va_mm, 1)
                if i == ITEMS:
                    xvalues(J1[:, :], 1)
                if i in (PROJ_I, PROJ_I + 1):
                    if i == PROJ_I:
                        pe.wait_ge(y_lo, 1)
                        pe.wait_ge(w_lo, PROJ_AT + 1)
                    for m in range(2):
                        pe.wait_ge((qh_sb, kh_sb)[m], i + 2)
                        project(2 * (i - PROJ_I) + m)
            pe.wait_ge(xv_sb, 1)
            xvalues(J0[:, :], 2)
            pe.wait_ge(xv_sb, 2)
            xvalues(J1[:, :], 3)
            pe.wait_ge(y_lo, 2)
            for b in range(HB, B):
                project(b)

            def xproj(dst, m, h, n):
                src = xt_r if m == "q" else ct_r
                for kt in range(KT):
                    ins = three(dst, lambda s: w_r[m][:, s, h, kt * P:(kt + 1) * P],
                                lambda s: src[:, s, kt, n * HALF:(n + 1) * HALF], kt == 0, kt == KT - 1)
                return ins

            def quarter(g, q, back, front):
                c = 8 * g + q
                h, n = q % GROUP, q // GROUP % 2
                hp, np_ = (q - 1) % GROUP, (q - 1) // GROUP % 2
                at = PER_GROUP * g + G0 + PER_GROUP * (q // 8)
                if front:
                    if n == 0:
                        pe.wait_ge(w_lo, at + SLOT["q"][h] + 1)
                    if front != "last" or q == GROUP:
                        pe.wait_ge(xv_sb, c + 4)
                    if front == "last" and q == 7:
                        pe.wait_ge(xt_hi, 2 * B + 2)
                    xproj(J0[:, :], "q", h, n).then_inc(xq_mm, 1)
                if back:
                    pe.wait_ge(xs_norm, c)
                    for b in range(HB):
                        ins = nc.tensor.transpose(TX[:, b * P:(b + 1) * P], scb[:, b, :], ident[:])
                    ins.then_inc(xt_mm, 1)
                if front:
                    if n == 0:
                        pe.wait_ge(w_lo, at + SLOT["k"][h] + 1)
                    xproj(J1[:, :], "k", h, n).then_inc(xk_mm, 1)
                if back and not front:
                    low_rank(0)
                if back:
                    pe.wait_ge(xp_sb, c)
                    for b in range(HB):
                        t = slice(b * P, (b + 1) * P)
                        ins = nc.tensor.matmul(TX[:, t], vals[:, np_, b, hp * P:(hp + 1) * P], pt[:, 0, t],
                                               start=True, stop=True)
                    ins.then_inc(xpv_mm, 1)
                if front:
                    pe.wait_ge(xq_sb, c + 1)
                    pe.wait_ge(xk_sb, c + 1)
                    for b in range(HB):
                        t = slice(b * P, (b + 1) * P)
                        ins = nc.tensor.matmul(SX[:, t], qt[:, t], kt_[:, t], start=True, stop=True)
                    ins.then_inc(xs_mm, 1)
                    if front != "last":
                        if q == GROUP:
                            pe.wait_ge(w_lo, at + PER_GROUP + GROUP)
                        xvalues(J0[:, :], HB * (1 - n) + h)
                    elif q in (6, 7):
                        adapter_turn(2 * q - 12)
                        adapter_turn(2 * q - 11)
                if back and not front:
                    router(0)
                if back:
                    if q <= GROUP:
                        pe.wait_ge(w_lo, at + SLOT["o"][hp] + 1)
                    if hp == 0:
                        pe.wait_ge(xo_add, B * g + B + HB * (q // GROUP))
                    pe.wait_ge(xo_lo, c)
                    for b in range(HB):
                        ins = three(OB[b][:, :], lambda s: r_o[:, s, b * P:(b + 1) * P],
                                    lambda s: w_r["o"][:, s, hp, :], hp == 0, hp == GROUP - 1)
                    ins.then_inc(xo_mm, 1)

            def second_turn(b):
                if b % HB >= 2:
                    pe.wait_ge(xt_lo, B + b - 1)
                tile_turn(B + b, hb[b % HB], bank[b % 2])

            for b in range(HB):
                second_turn(b)
            pe.wait_ge(xt_lo, B + HB)
            pe.wait_ge(pj_add, B)
            quarter(0, 0, False, True)
            for b in range(HB, B):
                second_turn(b)
            with pe.Fori(0, GROUPS - 1) as g:
                for q in range(1, 9):
                    quarter(g, q, True, True)
            def adapter_turn(b):
                tile_turn(2 * B + b, hb[b % HB], TURN[b])

            def low_rank(n):
                pe.wait_ge(xt_hi, 2 * B + HB * (n + 1))
                for j in range(HB):
                    for kt in range(KT):
                        nc.tensor.matmul(LOW[n][:, j * P:(j + 1) * P], vals[:, 0, j, kt * P:(kt + 1) * P],
                                         aws[:, kt, 0:P], start=kt == 0, stop=kt == KT - 1)

            def router(n):
                for j in range(HB):
                    for kt in range(KT):
                        ins = nc.tensor.matmul(ROUTE[n][:, j * E:(j + 1) * E], vals[:, 0, j, kt * P:(kt + 1) * P],
                                               aws[:, kt, P:P + E], start=kt == 0, stop=kt == KT - 1)
                ins.then_inc(ad_mm, 1)

            def combine(n):
                pe.wait_ge(g_rdy, n + 1)
                for j in range(HB):
                    ins = nc.tensor.transpose(GT[n][:, j * P:(j + 1) * P], bmrow[:, n, j * P:(j + 1) * P], ident[:])
                ins.then_inc(gt_mm, 1)
                pe.wait_ge(gt_sb, n + 1)
                for j in range(HB):
                    if n:
                        pe.wait_ge(f_add, j + 1)
                    nc.tensor.matmul(FB[j][:, :], kt_[:, j * P:(j + 1) * P], bws[:], start=True, stop=True)\
                        .then_inc(f_mm, 1)

            for q in range(1, 9):
                quarter(GROUPS - 1, q, True, False if q == 8 else "last" if q >= GROUP else True)
            combine(0)
            for b in range(HB, B):
                if b >= HB + 2:
                    pe.wait_ge(xt_hi, 2 * B + b - 1)
                adapter_turn(b)
            low_rank(1)
            router(1)
            combine(1)


N_CST = 9


def kernel(**inputs):
    import numpy as _np
    import concourse.bacc as _bacc
    from concourse import mybir as _mybir
    from concourse.bass_utils import run_bass_kernel_spmd as _run

    a = {k.replace("L0_", ""): _np.asarray(v) for k, v in inputs.items()}

    def heads(w):
        return w.reshape(XH, P, KT, P).transpose(0, 3, 2, 1).reshape(XH, P, D)

    xv = a["xattn_w_v"].reshape(GROUPS, D, KT, P).transpose(0, 2, 3, 1).reshape(XH, P, D)
    layout = {
        "x": a["x"],
        "ctx_t": a["ctx_4096"].reshape(TOK, D).T,
        "mask": a["mask_BxSxS2_bk0"],
        "conv_w": a["attn_conv_w"],
        "conv_b": a["attn_conv_b"].reshape(3, P).T,
        "wq": a["attn_wq"].reshape(P, 2 * D), "wk": a["attn_wk"].reshape(P, 2 * D), "wv": a["attn_wv"].reshape(P, 2 * D),
        "bq": a["attn_bq"].reshape(PAIRS, P).T, "bk": a["attn_bk"].reshape(PAIRS, P).T,
        "bv": a["attn_bv"].reshape(PAIRS, P).T,
        "wo": a["attn_wo"].reshape(2 * D, P),
        "bo": a["attn_bo"].reshape(P, 1),
        "proj_w": a["attn_proj_w"],
        "proj_b": a["attn_proj_b"],
        "pos": a["xattn_position_bias"],
        "lnw": a["xattn_ln_weight"],
        "xq": heads(a["xattn_w_q"]), "xk": heads(a["xattn_w_k"]), "xv": xv,
        "xo": a["xattn_w_out"].T.reshape(XH, P, D),
        "aw": _np.concatenate([a["ffn_A"].reshape(E * R, D).T, a["ffn_Wr"].T], axis=1),
        "bw": a["ffn_B"].transpose(0, 2, 1).reshape(E * R, D),
        "br": a["ffn_br"],
    }
    nc = _bacc.Bacc("TRN2", target_bir_lowering=False, num_devices=1)
    arrays, args = {}, []
    for name, v in layout.items():
        v = _np.ascontiguousarray(v)
        arrays[f"in_{name}"] = v
        args.append(nc.dram_tensor(f"in_{name}", v.shape, _mybir.dt.from_np(v.dtype), kind="ExternalInput").ap())
    args.append(nc.dram_tensor("out_x", (B, P, D), _mybir.dt.float32, kind="ExternalOutput").ap())
    decoder_layer(nc, *args)
    r = _run(nc, [arrays], core_ids=[0])
    return r.results[0]["out_x"]
```

```python
from contextlib import ExitStack

import concourse.bass as bass
from concourse import mybir

F32 = mybir.dt.float32
F32R = mybir.dt.float32r
BF16 = mybir.dt.bfloat16
I32 = mybir.dt.int32
U8 = mybir.dt.uint8
ALU = mybir.AluOpType
ACT = mybir.ActivationFunctionType
AX_X = mybir.AxisListType.X

P = 128
B = 8
D = 512
KT = D // P
TOK = B * P
HALF = TOK // 2
HB = B // 2
PAIRS = 8
ITEMS = 2 * PAIRS
XH = 32
GROUP = 4
GROUPS = XH // GROUP
E = 8
R = 16
PROJ_I = 10
PAD = P + 2
CONV = 3
CC = 3 * P
EPS = 1e-5
NEG = -1e9
MASKED = -1e30
BIG = 3e38
RING = 4
N_CONV = CONV * KT
WO_AT, PROJ_AT, CTX_AT = 6, 8, 9
G0 = CTX_AT + 2 * KT
PER_GROUP = 4 * GROUP
SLOT = {"v": [0, 1, 2, 3], "q": [4, 6, 9, 12], "k": [5, 7, 10, 13], "o": [8, 11, 14, 15]}
FIRST_SPLITS = [(8, 11), (11, 14), (14, 16)]
ORDER = sorted((i, m, h) for m, s in SLOT.items() for h, i in enumerate(s))


def decoder_layer(nc, x, ctx_t, mask, conv_w, conv_b, wq, wk, wv, bq, bk, bv, wo, bo, proj_w, proj_b,
                  pos, lnw, xq, xk, xv, xo, aw, bw, br, out):
    with ExitStack() as ctx:
        def sb(name, shape, dt=F32):
            return ctx.enter_context(nc.sbuf_tensor(name, shape, dt))

        def sem(name):
            return ctx.enter_context(nc.semaphore(name))

        r_a = sb("r_a", [P, 8192], F32R)
        r_x = sb("r_x", [P, 2 * KT * B * PAD], F32R)
        r_c = sb("r_c", [P, 2 * N_CONV * CC], F32R)
        r_q = sb("r_q", [P, 8192], F32R)
        r_o = sb("r_o", [P, 2, HALF], F32R)
        wqkv_r = r_a[:, 0:6144].rearrange("p (s m c) -> p s m c", s=2, m=3)
        wo_r = r_a[:, 6144:8192].rearrange("p (s c) -> p s c", s=2)
        xpad_r = r_x[:, :].rearrange("p (s k b t) -> p s k b t", s=2, k=KT, b=B)
        conv_r = r_c[:, :].rearrange("p (s j c) -> p s j c", s=2, j=N_CONV)
        proj_r = r_c[:, 8192:9216].rearrange("p (s c) -> p s c", s=2)
        qkv_r = r_q[:, 0:6144].rearrange("p (s m t) -> p s m t", s=2, m=3)
        ot_r = r_q[:, 6144:8192].rearrange("p (u s t) -> p u s t", u=2, s=2)
        yt_r = r_x[:, 0:2 * TOK].rearrange("p (s t) -> p s t", s=2)
        xt_r = r_x[:, 0:2 * KT * TOK].rearrange("p (s k t) -> p s k t", s=2, k=KT)
        ct_r = r_c[:, 0:8192].rearrange("p (s k t) -> p s k t", s=2, k=KT)
        w_r = {"q": r_a[:, 0:4096], "k": r_a[:, 4096:8192], "v": r_q[:, 0:4096], "o": r_q[:, 4096:8192]}
        w_r = {m: t.rearrange("p (s h c) -> p s h c", s=2, h=GROUP) for m, t in w_r.items()}

        acc = sb("acc", [P, B, D])
        vals = sb("vals", [P, 2, HB, D])
        va = vals[:, :, :, :].rearrange("p u b c -> p (u b c)").rearrange("p (b c) -> p b c", b=HB)
        qt = sb("qt", [P, HALF])
        kt_ = sb("kt", [P, HALF])
        sc = sb("sc", [P, 2, 2, HB, P])
        scb = sc[:, 0, 0, :, :]
        pt = sb("pt", [P, 2, HALF])
        hb = [sc[:, 0, 1, :, :].rearrange("p b k -> p (b k)"), sc[:, 1, 0, :, :].rearrange("p b k -> p (b k)"),
              sc[:, 1, 1, :, :].rearrange("p b k -> p (b k)"), pt[:, 1, :]]
        bm = sb("bm", [P, 2, HB, P])
        bmrow = bm[:, :, :, :].rearrange("p u b k -> p u (b k)")
        projb_b, lnw_b = bmrow[:, 0, :], bmrow[:, 1, :]
        maskb = sb("maskb", [P, B, P], BF16)
        mask_u = sb("mask_u", [P, B, P], U8)
        anyv = sb("anyv", [P, B])
        pb = sb("pb", [P, GROUP, P])
        ring = sb("ring", [P, RING, D])
        ident = sb("ident", [P, P])
        causal = sb("causal", [P, P])
        cb = sb("cb", [P, 3])
        bqs, bks, bvs, bos = sb("bqs", [P, PAIRS]), sb("bks", [P, PAIRS]), sb("bvs", [P, PAIRS]), sb("bos", [P, 1])
        aws = sb("aws", [P, KT, P + E])
        bws = sb("bws", [P, D])
        brs = sb("brs", [P, E])
        st = sb("st", [P, B, 6])
        mv = sb("mv", [P, B, 2])
        ve = sb("ve", [P, B])
        rs = sb("rs", [P, B])
        nt = sb("nt", [P, B])
        r1, mr, u1, mu = sb("r1", [P, B]), sb("mr", [P, B]), sb("u1", [P, B]), sb("mu", [P, B])
        nmx = sb("nmx", [P, 2, 8])
        sums = sb("sums", [P, 2, 8])
        rinv = sb("rinv", [P, 8])
        scratch = sb("scratch", [P, 1])
        lg = sb("lg", [P, HB, E])
        lmx = sb("lmx", [P, HB])
        lsum = sb("lsum", [P, HB])
        lr = sb("lr", [P, HB])
        scw = sb("scw", [P, HB, E])

        bank = [ctx.enter_context(nc.psum_tensor(f"bank{i}", [P, 512], F32)) for i in range(8)]
        h1 = [pt[:, 0, :], pt[:, 1, :], qt[:, :], kt_[:, :]]
        NB = [bank[0], bank[1], bank[5], bank[6]]
        S2, T2, PVB, J0, J1, Y = bank[0:2], bank[2:4], bank[4], bank[5], bank[6], bank[7]
        OB, SX, TX = bank[0:4], bank[4], bank[7]
        CB = [bank[2], bank[3], bank[4], bank[0], bank[1], bank[7]]
        LOW, GT = [[J0, J1], [bank[2], bank[1]]], [[bank[4], bank[7]], [bank[0], bank[3]]]
        FB = [J0, J1, bank[7], bank[4]]
        VB = [[bank[2], bank[3], bank[4], bank[7], J0, J1, bank[2], bank[3]], [bank[2], bank[3], J0, J1] * 2]
        XB = [bank[0], bank[1], bank[0], bank[1]] + bank[0:4]
        TURN = [J0, J1] * 2 + [bank[0], bank[1]] * 2
        PJ = [J0, J1, J0, J1, bank[2], bank[3], bank[4], bank[7]]

        x_ld = [sem(f"x_ld{n}") for n in range(HB + 1)]
        cst_ld, mask_ld, lnw_ld = sem("cst_ld"), sem("mask_ld"), sem("lnw_ld")
        w_ld = [sem(f"w_ld{i}") for i in range(RING)]
        pb_ld = [sem(f"pb_ld{h}") for h in range(GROUP)]
        w_hi, w_lo = sem("w_hi"), sem("w_lo")
        tap_ld = [sem(f"tap_ld{t}") for t in range(CONV)]
        tap_hi, tap0_lo, tap_lo = sem("tap_hi"), sem("tap0_lo"), sem("tap_lo")
        id_rdy, cz_rdy, pads_rdy, projb_add, mask_rdy, any_rdy = (
            sem("id_rdy"), sem("cz_rdy"), sem("pads_rdy"), sem("projb_add"), sem("mask_rdy"), sem("any_rdy"))
        st_rdy, xn_rdy, tp_mm, xt_hi, xt_lo, u_rdy, h_rdy = (
            sem("st_rdy"), sem("xn_rdy"), sem("tp_mm"), sem("xt_hi"), sem("xt_lo"), sem("u_rdy"), sem("h_rdy"))
        cv_mm, cv_hi, cv_lo = sem("cv_mm"), sem("cv_hi"), sem("cv_lo")
        qh_mm, kh_mm, qh_sb, kh_sb = sem("qh_mm"), sem("kh_mm"), sem("qh_sb"), sem("kh_sb")
        va_mm, va_even, va_odd = sem("va_mm"), sem("va_even"), sem("va_odd")
        s_mm, s_max, s_exp, s_rcp, s_even, s_odd = (
            sem("s_mm"), sem("s_max"), sem("s_exp"), sem("s_rcp"), sem("s_even"), sem("s_odd"))
        t_mm, pt_even, pt_odd, pv_mm, o_hi, o_lo, wo_mm, y_hi, y_lo, pj_mm, pj_add = (
            sem("t_mm"), sem("pt_even"), sem("pt_odd"), sem("pv_mm"), sem("o_hi"), sem("o_lo"), sem("wo_mm"),
            sem("y_hi"), sem("y_lo"), sem("pj_mm"), sem("pj_add"))
        xv_mm, xv_sb, xq_mm, xq_sb, xk_mm, xk_sb = (
            sem("xv_mm"), sem("xv_sb"), sem("xq_mm"), sem("xq_sb"), sem("xk_mm"), sem("xk_sb"))
        xs_mm, xs_max, xs_exp, xs_rcp, xs_norm, bm_rdy = (
            sem("xs_mm"), sem("xs_max"), sem("xs_exp"), sem("xs_rcp"), sem("xs_norm"), sem("bm_rdy"))
        xt_mm, xp_sb, xpv_mm, xo_hi, xo_lo, xo_mm, xo_add = (
            sem("xt_mm"), sem("xp_sb"), sem("xpv_mm"), sem("xo_hi"), sem("xo_lo"), sem("xo_mm"), sem("xo_add"))
        low_mm, lg_rdy, lg_exp, g_rdy, gt_mm, gt_sb, f_mm, f_add, out_st = (
            sem("low_mm"), sem("lg_rdy"), sem("lg_exp"), sem("g_rdy"), sem("gt_mm"), sem("gt_sb"),
            sem("f_mm"), sem("f_add"), sem("out_st"))
        dve_seq = sem("dve_seq")

        cw_v = conv_w.rearrange("t (k p) c -> p t k c", p=P)
        tap_raw = [sc[:, :, :, :, :].rearrange("p u e b k -> p (u e b k)")[:, 0:KT * CC],
                   va[:, :, :].rearrange("p b c -> p (b c)")[:, 0:KT * CC],
                   va[:, :, :].rearrange("p b c -> p (b c)")[:, KT * CC:2 * KT * CC]]
        tap_r = r_c[:, :].rearrange("p (s t c) -> p s t c", s=2, t=CONV)
        staged = []
        for m, w in enumerate((wq, wk, wv)):
            for s in range(2):
                c = slice(s * D, s * D + D)
                staged.append((w[:, c], wqkv_r[:, 0, m, c], wqkv_r[:, 1, m, c], D))
        wo_v = wo.rearrange("(j p) c -> p j c", p=P)
        for s in range(2):
            c = slice(s * D, s * D + D)
            staged.append((wo_v[:, 4 * s:4 * s + 4, :], wo_r[:, 0, c], wo_r[:, 1, c], D))
        staged.append((proj_w, proj_r[:, 0, :], proj_r[:, 1, :], D))
        for k in range(KT):
            for n in range(2):
                c = slice(n * HALF, n * HALF + HALF)
                staged.append((ctx_t[k * P:(k + 1) * P, c], ct_r[:, 0, k, c], ct_r[:, 1, k, c], HALF))
        assert len(staged) == G0
        xw = {"q": xq, "k": xk, "v": xv, "o": xo}

        def slot_of(pos):
            return pos % RING

        def group_item(j):
            _, m, h = ORDER[j]
            return m, h, w_r[m][:, 0, h, :], w_r[m][:, 1, h, :]

        def pos_v(first, h):
            return pos[bass.ds(first + h, 1), :, :].rearrange("a q k -> (a q) k")

        block = ctx.enter_context(nc.Block())

        @block.sync
        def _(sp):
            def load_static(pos, src, cols):
                if pos >= RING:
                    sp.wait_ge(w_lo, pos - RING + 1)
                dst = ring[:, slot_of(pos), 0:cols]
                if len(src.shape) == 3:
                    dst = dst.rearrange("p (j c) -> p j c", j=src.shape[1])
                sp.dma_start(dst, src).then_inc(w_ld[slot_of(pos)], 16)

            xv_ = x.rearrange("b t d -> t b d")
            for b in range(HB):
                sp.dma_start(acc[:, b, :], xv_[:, b, :]).then_inc(x_ld[b], 16)
            for t in range(CONV):
                sp.dma_start(tap_raw[t].rearrange("p (k c) -> p k c", k=KT), cw_v[:, t, :, :]).then_inc(tap_ld[t], 16)
            sp.dma_start(acc[:, HB:B, :], xv_[:, HB:B, :]).then_inc(x_ld[HB], 16)
            for pos, (src, _, _, cols) in enumerate(staged):
                load_static(pos, src, cols)
            for h in range(GROUP):
                sp.dma_start(pb[:, h, :], pos_v(0, h)).then_inc(pb_ld[h], 16)
            for j in range(PER_GROUP):
                m, h, _, _ = group_item(j)
                load_static(G0 + j, xw[m][h], D)

            with sp.Fori(0, GROUPS - 1) as g:
                for j in range(PER_GROUP):
                    m, h, _, _ = group_item(j)
                    if m == "q":
                        sp.wait_ge(bm_rdy, 8 * g + 4 + h + 1)
                        sp.dma_start(pb[:, h, :], pos_v((g + 1) * GROUP, h)).then_inc(pb_ld[h], 16)
                    pos = G0 + PER_GROUP + j
                    sp.wait_ge(w_lo, PER_GROUP * g + pos - RING + 1)
                    src = xw[m][bass.ds((g + 1) * GROUP + h, 1), :, :].rearrange("a p c -> (a p) c")
                    sp.dma_start(ring[:, slot_of(pos), :], src).then_inc(w_ld[slot_of(pos)], 16)

            for b in range(B):
                sp.wait_ge(f_add, b + 1)
                sp.dma_start(out[b], acc[:, b, :]).then_inc(out_st, 16)
            sp.wait_ge(out_st, 16 * B)

        @block.gpsimd
        def _(pool):
            def split_hi(pos, dst, cols):
                pool.wait_ge(w_ld[slot_of(pos)], 16 * (pos // RING + 1))
                nc.gpsimd.tensor_copy(dst, ring[:, slot_of(pos), 0:cols]).then_inc(w_hi, 1)

            nc.gpsimd.memset(ident[:], 0.0).then_inc(cz_rdy, 1)
            nc.gpsimd.memset(causal[:], 0.0).then_inc(cz_rdy, 1)
            nc.gpsimd.memset(xpad_r[:, :, :, :, 0:PAD:PAD - 1].bitcast(F32)
                             .rearrange("p s k b t -> p (s k b) t"), 0.0).then_inc(pads_rdy, 1)
            pool.wait_ge(cz_rdy, 2)
            nc.gpsimd.affine_select(out=ident[:], in_=ident[:], compare_op=ALU.not_equal, fill=1.0, base=0,
                                    pattern=[[-1, P]], channel_multiplier=1).then_inc(id_rdy, 1)
            nc.gpsimd.affine_select(out=causal[:], in_=causal[:], compare_op=ALU.is_ge, fill=NEG, base=0,
                                    pattern=[[-1, P]], channel_multiplier=1).then_inc(id_rdy, 1)
            pool.wait_ge(tap_hi, 1)
            nc.gpsimd.tensor_tensor(tap_r[:, 1, 0, :], tap_raw[0], tap_r[:, 0, 0, :].bitcast(F32), ALU.subtract)\
                .then_inc(tap0_lo, 1)
            for p_ in range(WO_AT + 2):
                _, hi, _, cols = staged[p_]
                split_hi(p_, hi, cols)
            pool.wait_ge(cst_ld, 16 * N_CST)
            pool.wait_ge(xn_rdy, B)
            for b in range(B):
                nc.gpsimd.tensor_tensor(acc[:, b, :], acc[:, b, :], projb_b, ALU.add).then_inc(projb_add, 1)
            pool.wait_ge(mask_ld, 16)
            nc.gpsimd.tensor_scalar(maskb[:, :, :], mask_u[:, :, :], 1.0, -MASKED, ALU.subtract, ALU.mult)\
                .then_inc(mask_rdy, 1)

            def bias_mask(c, q):
                h, n = q % GROUP, q // GROUP % 2
                pool.wait_ge(pb_ld[h], 16 * c[1] + 16)
                nc.gpsimd.tensor_tensor(bm[:, q % 2, :, :], maskb[:, HB * n:HB * n + HB, :],
                                        pb[:, h, :].unsqueeze(1).broadcast_to((P, HB, P)), ALU.add)\
                    .then_inc(bm_rdy, 1)

            pool.wait_ge(cv_mm, 6)
            for i in range(ITEMS):
                pool.wait_ge(s_rcp, 2 * i + 1)
                t = sc[:, i % 2, 0, :, :]
                nc.gpsimd.tensor_tensor(t, t, rinv[:, 0:HB].unsqueeze(2).broadcast_to((P, HB, P)), ALU.mult)\
                    .then_inc(s_even, 1)
                if PROJ_AT + i < G0:
                    _, hi, _, cols = staged[PROJ_AT + i]
                    split_hi(PROJ_AT + i, hi, cols)
                if i >= ITEMS - 2:
                    for h in range(2 * (i - ITEMS + 2), 2 * (i - ITEMS + 2) + 2):
                        pos = G0 + h
                        _, _, hi, lo = group_item(h)
                        pool.wait_ge(w_hi, pos + 1)
                        nc.gpsimd.tensor_tensor(lo, ring[:, slot_of(pos), :], hi.bitcast(F32), ALU.subtract)\
                            .then_inc(w_lo, 1)

            pool.wait_ge(mask_rdy, 1)
            pool.wait_ge(projb_add, B)
            bias_mask((0, 0), 0)
            def residual(b):
                pool.wait_ge(h_rdy, b + 1)
                nc.gpsimd.tensor_scalar(acc[:, b, :], acc[:, b, :], r1[:, b:b + 1], mr[:, b:b + 1],
                                        ALU.mult, ALU.subtract).then_inc(xo_add, 1)
            for b in range(HB):
                residual(b)
            pool.wait_ge(xn_rdy, 2 * B)
            bias_mask((1, 0), 1)

            def group(g, first, last):
                for q in range(1, 9):
                    c = 8 * g + q
                    if not last or q < 7:
                        pool.wait_ge(xs_max, 4 * c)
                        bias_mask((c + 1, g + (q + 1) // 8), (q + 1) % 8)
                    if first and q <= HB:
                        residual(HB + q - 1)

            group(0, True, False)
            with pool.Fori(1, GROUPS - 1) as g:
                group(g, False, False)
            group(GROUPS - 1, False, True)

        @block.scalar
        def _(act):
            def split_hi(pos):
                act.wait_ge(w_ld[slot_of(pos)], 16 * (pos // RING + 1))
                nc.scalar.activation(group_item(pos - G0)[2], ring[:, slot_of(pos), :], ACT.Copy).then_inc(w_hi, 1)

            def tile_hi(b):
                act.wait_ge(tp_mm, b + 1)
                nc.scalar.activation(xpad_r[:, 0, :, b, 1:1 + P],
                                     NB[b % HB][:, :].rearrange("p (k t) -> p k t", k=KT), ACT.Copy)\
                    .then_inc(xt_hi, 1)

            def tap_hi_out(t):
                act.wait_ge(tap_ld[t], 16)
                nc.scalar.activation(tap_r[:, 0, t, :], tap_raw[t], ACT.Copy).then_inc(tap_hi, 1)

            tap_hi_out(0)
            for b in range(HB):
                tile_hi(b)
            tap_hi_out(1)
            tap_hi_out(2)
            small = [(cb[:], conv_b), (bqs[:], bq), (bks[:], bk), (bvs[:], bv), (bos[:], bo),
                     (projb_b, proj_b.partition_broadcast(P)), (aws[:, :, :], aw.rearrange("(k p) c -> p k c", p=P)),
                     (bws[:], bw), (brs[:], br.partition_broadcast(P))]
            assert len(small) == N_CST
            for dst, src in small:
                act.dma_start(dst, src).then_inc(cst_ld, 16)
            act.dma_start(lnw_b, lnw.partition_broadcast(P)).then_inc(lnw_ld, 16)
            act.dma_start(mask_u[:, :, :], mask.rearrange("b q k -> q b k")).then_inc(mask_ld, 16)

            def conv_hi(j):
                n, m = divmod(j, 3)
                act.wait_ge(cv_mm, j + 1)
                nc.scalar.activation(qkv_r[:, 0, m, n * HALF:(n + 1) * HALF], CB[j][:, :], ACT.Identity,
                                     bias=cb[:, m:m + 1]).then_inc(cv_hi, 1)

            act.wait_ge(cst_ld, 16 * N_CST)
            conv_hi(0)
            for b in range(HB, B):
                tile_hi(b)
            conv_hi(1)
            for j in range(2, 5):
                conv_hi(j)

            def kh_out(i):
                act.wait_ge(kh_mm, i + 1)
                nc.scalar.activation(kt_[:], J1[:, :], ACT.Identity, bias=bks[:, i % PAIRS:i % PAIRS + 1])\
                    .then_inc(kh_sb, 1)

            def values_split(a, z):
                act.wait_ge(kh_mm, ITEMS)
                for s in range(a, z):
                    split_hi(G0 + s)

            def pt_out(i):
                act.wait_ge(t_mm, i)
                nc.scalar.copy(pt[:, 0, :], T2[0][:, :]).then_inc(pt_even, 1)

            def row_norm(b):
                if b % HB == 0:
                    act.wait_ge(u_rdy, b // HB + 1)
                if b >= HB:
                    act.wait_ge(tp_mm, B + b - HB + 1)
                nc.scalar.activation(hb[b % HB], acc[:, b, :], ACT.Identity, bias=mu[:, b:b + 1],
                                     scale=u1[:, b:b + 1]).then_inc(h_rdy, 1)

            def value(b):
                act.wait_ge(xv_mm, b + 1)
                nc.scalar.copy(vals[:, 0, b, :], (J0, J1)[b % 2][:, :]).then_inc(xv_sb, 1)

            def xtile_hi(b):
                act.wait_ge(tp_mm, B + b + 1)
                nc.scalar.activation(xt_r[:, 0, :, b * P:(b + 1) * P],
                                     XB[b][:, :].rearrange("p (k t) -> p k t", k=KT), ACT.Copy)\
                    .then_inc(xt_hi, 1)

            kh_out(0)
            conv_hi(5)
            for i in range(ITEMS + 2):
                for e in range(2):
                    if e == 1 and i + 1 < ITEMS:
                        kh_out(i + 1)
                    if e == 1 and i == ITEMS - 1:
                        values_split(2, 3)
                    if i < ITEMS:
                        for b in range(HB):
                            k = 4 * e + b
                            if k == 2 and i >= 1:
                                pt_out(i)
                            act.wait_ge(s_max, 8 * i + k + 1)
                            t = sc[:, i % 2, e, b, :]
                            nc.scalar.activation(t, t, ACT.Exp, scale=-1.0, bias=nmx[:, i % 2, k:k + 1],
                                                 accum_out=sums[:, i % 2, k:k + 1]).then_inc(s_exp, 1)
                    elif i == ITEMS and e == 0:
                        pt_out(i)
                if i == ITEMS + 1:
                    row_norm(0)
                    row_norm(1)
                if i - 2 in (PAIRS - 1, ITEMS - 1):
                    n = (i - 2) // PAIRS
                    act.wait_ge(wo_mm, i - 1)
                    nc.scalar.activation(yt_r[:, 0, n * HALF:(n + 1) * HALF], Y[:, :], ACT.Identity,
                                         bias=bos[:, 0:1]).then_inc(y_hi, 1)
                if i == ITEMS:
                    act.wait_ge(xv_mm, 1)
                    nc.scalar.copy(vals[:, 0, 0, :], J0[:, :]).then_inc(xv_sb, 1)
                if 1 <= i <= ITEMS:
                    act.wait_ge(pv_mm, i)
                    p_ = (i - 1) % PAIRS
                    nc.scalar.activation(ot_r[:, (i - 1) % 2, 0, :], PVB[:, :], ACT.Identity,
                                         bias=bvs[:, p_:p_ + 1]).then_inc(o_hi, 1)
                if i % PAIRS == 0 and i < ITEMS:
                    for m in range(0, B, 2):
                        act.wait_ge(va_mm, i + m + 1)
                        nc.scalar.copy(va[:, m // 2, 0:D], VB[i // PAIRS][m][:, :]).then_inc(va_even, 1)
                if i == ITEMS - 2:
                    values_split(0, 2)
                if i == ITEMS - 1:
                    values_split(3, 4)

            def first_quarters_split(a, z):
                act.wait_ge(wo_mm, ITEMS)
                for j in range(a, z):
                    split_hi(G0 + j)

            value(1)
            row_norm(2)
            row_norm(3)
            xtile_hi(0)
            xtile_hi(1)
            first_quarters_split(4, 6)
            value(2)
            xtile_hi(2)
            xtile_hi(3)
            value(3)
            first_quarters_split(6, 8)

            def quarter(c, q, back, front):
                if front:
                    act.wait_ge(xq_mm, c + 1)
                    nc.scalar.copy(qt[:], J0[:, :]).then_inc(xq_sb, 1)
                if back:
                    act.wait_ge(xt_mm, c)
                    nc.scalar.copy(pt[:, 0, :], TX[:, :]).then_inc(xp_sb, 1)
                if front:
                    act.wait_ge(xk_mm, c + 1)
                    nc.scalar.copy(kt_[:], J1[:, :]).then_inc(xk_sb, 1)
                if isinstance(c, int) and c == 1:
                    for b in range(HB, B):
                        xtile_hi(b)
                if back and not front:
                    gates(0, 0)
                if back:
                    act.wait_ge(xpv_mm, c)
                    nc.scalar.activation(r_o[:, 0, :], TX[:, :], ACT.Copy).then_inc(xo_hi, 1)
                if front:
                    for b in range(HB):
                        act.wait_ge(xs_max, 4 * c + b + 1)
                        t = scb[:, b, :]
                        nc.scalar.activation(t, t, ACT.Exp, scale=-1.0, bias=nmx[:, 0, b:b + 1],
                                             accum_out=sums[:, 0, b:b + 1]).then_inc(xs_exp, 1)
                    if front != "last":
                        act.wait_ge(xv_mm, c + 5)
                        u = (q // GROUP + 1) % 2
                        nc.scalar.copy(vals[:, u, q % GROUP, :], J0[:, :]).then_inc(xv_sb, 1)

            quarter(0, 0, False, True)
            first_quarters_split(*FIRST_SPLITS[0])
            for b in range(HB, B):
                row_norm(b)
            for q in range(1, 9):
                quarter(q, q, True, True)
                if q < len(FIRST_SPLITS):
                    first_quarters_split(*FIRST_SPLITS[q])
            with act.Fori(1, GROUPS - 1) as g:
                for q in range(1, 9):
                    quarter(8 * g + q, q, True, True)

            def atile(b):
                act.wait_ge(tp_mm, 2 * B + b + 1)
                nc.scalar.copy(vals[:, 0, b % HB, :], TURN[b][:, :]).then_inc(xt_hi, 1)

            def gates(n, u):
                act.wait_ge(lg_rdy, 2 * n + u + 1)
                t = lg[:, 2 * u:2 * u + 2, :]
                nc.scalar.activation(t, t, ACT.Exp).then_inc(lg_exp, 1)

            def turned(n):
                if n:
                    act.wait_ge(f_mm, HB)
                for u in range(2):
                    act.wait_ge(gt_mm, 2 * n + u + 1)
                    nc.scalar.copy(kt_[:, u * 2 * P:(u + 1) * 2 * P], GT[n][u][:, 0:2 * P]).then_inc(gt_sb, 1)

            for q in range(1, 9):
                quarter(8 * (GROUPS - 1) + q, q, True, False if q == 8 else "last" if q >= 4 else True)
                if q in (6, 7):
                    atile(2 * q - 12)
                    atile(2 * q - 11)
            gates(0, 1)
            turned(0)
            for b in range(HB, B):
                atile(b)
            gates(1, 0)
            gates(1, 1)
            turned(1)

        @block.vector
        def _(dve):
            done = [0]

            def link(ins):
                done[0] += 1
                ins.then_inc(dve_seq, 1)
                dve.wait_ge(dve_seq, done[0])

            def split_lo(pos, base, hi, lo, cols):
                dve.wait_ge(w_hi, base + pos + 1)
                nc.vector.tensor_tensor(lo, ring[:, slot_of(pos), 0:cols], hi.bitcast(F32), ALU.subtract)\
                    .then_inc(w_lo, 1)

            def split_static(a, z):
                for p_ in range(a, z):
                    if p_ < G0:
                        _, hi, lo, cols = staged[p_]
                        split_lo(p_, 0, hi, lo, cols)
                    else:
                        _, _, hi, lo = group_item(p_ - G0)
                        split_lo(p_, 0, hi, lo, D)

            def rsqrt(cols):
                v, r, t = ve[:, cols], rs[:, cols], nt[:, cols]
                link(nc.vector.tensor_scalar(r.bitcast(I32), v.bitcast(I32), 1, None, ALU.logical_shift_right))
                link(nc.vector.tensor_scalar(r.bitcast(I32), r.bitcast(I32), -1.0, float(0x5F3759DF), ALU.mult, ALU.add))
                for _ in range(3):
                    link(nc.vector.tensor_tensor(t, r, r, ALU.mult))
                    link(nc.vector.scalar_tensor_tensor(t, t, -0.5, v, ALU.mult, ALU.mult))
                    link(nc.vector.scalar_tensor_tensor(r, t, 1.5, r, ALU.add, ALU.mult))

            def stats(b):
                nc.vector.bn_stats(st[:, b, :], acc[:, b, :]).then_inc(st_rdy, 1)

            def moments(n, turn=1):
                dve.wait_ge(st_rdy, B * turn + HB * (n + 1))
                for b in range(HB * n, HB * n + HB):
                    ins = nc.vector.bn_aggr(mv[:, b, :], st[:, b, :])
                link(ins)
                cols = slice(HB * n, HB * n + HB)
                link(nc.vector.tensor_scalar(ve[:, cols], mv[:, cols, 1], EPS, None, ALU.add))
                rsqrt(cols)

            def centre(dst, b):
                return nc.vector.tensor_scalar(dst, acc[:, b, :], mv[:, b, 0:1], rs[:, b:b + 1],
                                               ALU.subtract, ALU.mult)

            def tile_lo(k, dst, hi, src):
                dve.wait_ge(xt_hi, k + 1)
                src = src[:, :].rearrange("p (k t) -> p k t", k=KT)
                nc.vector.tensor_tensor(dst, src, hi.bitcast(F32), ALU.subtract).then_inc(xt_lo, 1)

            def norm_tile(b):
                if b >= HB:
                    dve.wait_ge(tp_mm, b - HB + 1)
                centre(h1[b % HB], b).then_inc(xn_rdy, 1)

            def norm_lo(b):
                tile_lo(b, xpad_r[:, 1, :, b, 1:1 + P], xpad_r[:, 0, :, b, 1:1 + P], NB[b % HB])

            def tap_rest(t):
                dve.wait_ge(tap_hi, t + 1)
                nc.vector.tensor_tensor(tap_r[:, 1, t, :], tap_raw[t], tap_r[:, 0, t, :].bitcast(F32), ALU.subtract)\
                    .then_inc(tap_lo, 1)

            def conv_rest(j):
                n, m = divmod(j, 3)
                t = slice(n * HALF, (n + 1) * HALF)
                dve.wait_ge(cv_hi, j + 1)
                nc.vector.scalar_tensor_tensor(qkv_r[:, 1, m, t], CB[j][:, :], cb[:, m:m + 1],
                                               qkv_r[:, 0, m, t].bitcast(F32), ALU.add, ALU.subtract)\
                    .then_inc(cv_lo, 1)

            dve.wait_ge(pads_rdy, 1)
            for b in range(HB):
                dve.wait_ge(x_ld[b], 16)
                stats(b)
            moments(0, 0)
            for b in range(HB):
                norm_tile(b)
            for b in range(HB):
                norm_lo(b)
            tap_rest(1)
            tap_rest(2)
            dve.wait_ge(x_ld[HB], 16)
            for b in range(HB, B):
                stats(b)
            moments(1, 0)
            for b in range(HB, B):
                norm_tile(b)
            dve.wait_ge(cst_ld, 16 * N_CST)
            split_static(0, RING)
            conv_rest(0)
            for b in range(HB, B):
                norm_lo(b)
            split_static(RING, WO_AT)
            conv_rest(1)
            for j in range(2, 5):
                conv_rest(j)
            split_static(WO_AT, WO_AT + 2)

            def qh_out(i):
                dve.wait_ge(qh_mm, i + 1)
                nc.vector.tensor_scalar(qt[:], J0[:, :], bqs[:, i % PAIRS:i % PAIRS + 1], 0.125,
                                        ALU.add, ALU.mult).then_inc(qh_sb, 1)

            def group_rest(a, z):
                split_static(G0 + a, G0 + z)

            def project_add(b):
                dve.wait_ge(pj_mm, b + 1)
                nc.vector.tensor_tensor(acc[:, b, :], acc[:, b, :], PJ[b][:, :], ALU.add).then_inc(pj_add, 1)

            def rms(n):
                cols = slice(HB * n, HB * n + HB)
                v, r = mv[:, cols, 1], rs[:, cols]
                nc.vector.tensor_scalar(r1[:, cols], r, 1.0, None, ALU.add)
                nc.vector.tensor_tensor(mr[:, cols], mv[:, cols, 0], r, ALU.mult)
                link(nc.vector.tensor_tensor(u1[:, cols], r, r, ALU.mult))
                link(nc.vector.tensor_tensor(ve[:, cols], u1[:, cols], v, ALU.mult))
                link(nc.vector.tensor_scalar(ve[:, cols], ve[:, cols], EPS, None, ALU.add))
                link(nc.vector.tensor_copy(u1[:, cols], r))
                rsqrt(cols)
                link(nc.vector.tensor_tensor(u1[:, cols], u1[:, cols], r, ALU.mult))
                nc.vector.scalar_tensor_tensor(mu[:, cols], mv[:, cols, 0], -1.0, u1[:, cols], ALU.mult, ALU.mult)\
                    .then_inc(u_rdy, 1)

            def row_out(b):
                j = b % HB
                if b == 0:
                    dve.wait_ge(lnw_ld, 16)
                dve.wait_ge(h_rdy, b + 1)
                nc.vector.tensor_tensor(hb[j], hb[j], lnw_b, ALU.mult).then_inc(xn_rdy, 1)

            def xtile_rest(b):
                t = slice(b * P, (b + 1) * P)
                tile_lo(B + b, xt_r[:, 1, :, t], xt_r[:, 0, :, t], XB[b])

            qh_out(0)
            conv_rest(5)
            dve.wait_ge(id_rdy, 2)
            dve.wait_ge(projb_add, B)
            def pt_out(i):
                dve.wait_ge(t_mm, i)
                nc.vector.tensor_copy(pt[:, 1, :], T2[1][:, :]).then_inc(pt_odd, 1)

            dve.wait_ge(mask_ld, 16)
            nc.vector.tensor_reduce(anyv[:], mask_u[:, :, :], AX_X, ALU.max).then_inc(any_rdy, 1)
            dve.wait_ge(any_rdy, 1)
            for i in range(ITEMS + 2):
                if i < ITEMS:
                    dve.wait_ge(s_mm, i + 1)
                    for k in range(8):
                        e, b = divmod(k, HB)
                        if k == 6 and i >= 1:
                            pt_out(i)
                        nc.vector.tensor_tensor_reduce(
                            sc[:, i % 2, e, b, :], S2[e][:, b * P:(b + 1) * P], causal[:], -1.0, BIG,
                            ALU.add, ALU.min, nmx[:, i % 2, k:k + 1]).then_inc(s_max, 1)
                if i == ITEMS:
                    pt_out(i)
                if i + 1 < ITEMS:
                    qh_out(i + 1)
                if i < ITEMS:
                    for e in range(2):
                        k = slice(4 * e, 4 * e + 4)
                        dve.wait_ge(s_exp, 8 * i + 4 * e + 4)
                        nc.vector.reciprocal(rinv[:, k], sums[:, i % 2, k]).then_inc(s_rcp, 1)
                        if e:
                            dve.wait_ge(s_rcp, 2 * i + 2)
                            t = sc[:, i % 2, 1, :, :]
                            nc.vector.tensor_tensor(t, t, rinv[:, k].unsqueeze(2).broadcast_to((P, HB, P)),
                                                    ALU.mult).then_inc(s_odd, 1)
                        if e == 0 and 1 <= i <= G0 - PROJ_AT:
                            split_static(PROJ_AT + i - 1, PROJ_AT + i)
                        if e == 0 and ITEMS - HB <= i:
                            row = i - ITEMS + HB
                            dve.wait_ge(pj_add, row + 1)
                            stats(row)
                if i == ITEMS:
                    moments(0)
                    rms(0)
                if i - 2 in (PAIRS - 1, ITEMS - 1):
                    n = (i - 2) // PAIRS
                    t = slice(n * HALF, (n + 1) * HALF)
                    dve.wait_ge(y_hi, n + 1)
                    nc.vector.scalar_tensor_tensor(yt_r[:, 1, t], Y[:, :], bos[:, 0:1],
                                                   yt_r[:, 0, t].bitcast(F32), ALU.add, ALU.subtract)\
                        .then_inc(y_lo, 1)
                if 1 <= i <= ITEMS:
                    p_, u = (i - 1) % PAIRS, (i - 1) % 2
                    dve.wait_ge(o_hi, i)
                    nc.vector.scalar_tensor_tensor(ot_r[:, u, 1, :], PVB[:, :], bvs[:, p_:p_ + 1],
                                                   ot_r[:, u, 0, :].bitcast(F32), ALU.add, ALU.subtract)\
                        .then_inc(o_lo, 1)
                if i % PAIRS == 0 and i < ITEMS:
                    for m in range(1, B, 2):
                        dve.wait_ge(va_mm, i + m + 1)
                        nc.vector.tensor_copy(va[:, m // 2, D:2 * D], VB[i // PAIRS][m][:, :]).then_inc(va_odd, 1)
                if i in (PROJ_I, PROJ_I + 1):
                    project_add(2 * (i - PROJ_I))
                    project_add(2 * (i - PROJ_I) + 1)
                if i == ITEMS:
                    row_out(0)
                    row_out(1)
            def end_row(b):
                project_add(b)
                dve.wait_ge(pj_add, b + 1)
                stats(b)

            row_out(2)
            row_out(3)
            xtile_rest(0)
            xtile_rest(1)
            dve.wait_ge(w_lo, G0 + GROUP)
            group_rest(4, 6)
            end_row(4)
            xtile_rest(2)
            xtile_rest(3)
            for b in range(5, B):
                end_row(b)


            def quarter(c, q, back, front):
                if back:
                    dve.wait_ge(xo_hi, c)
                    nc.vector.tensor_tensor(r_o[:, 1, :], TX[:, :], r_o[:, 0, :].bitcast(F32), ALU.subtract)\
                        .then_inc(xo_lo, 1)
                if front:
                    n = q // GROUP % 2
                    dve.wait_ge(xs_mm, c + 1)
                    dve.wait_ge(bm_rdy, c + 1)
                    nc.vector.memset(scratch[:], 0.0)
                    for b in range(HB):
                        nc.vector.tensor_tensor_reduce(
                            scb[:, b, :], SX[:, b * P:(b + 1) * P], bm[:, q % 2, b, :], -1.0, BIG,
                            ALU.add, ALU.min, nmx[:, 0, b:b + 1]).then_inc(xs_max, 1)
                    dve.wait_ge(xs_exp, 4 * c + 4)
                    nc.vector.reciprocal(rinv[:, 0:HB], sums[:, 0, 0:HB]).then_inc(xs_rcp, 1)
                    dve.wait_ge(xs_rcp, 2 * c + 1)
                    nc.vector.tensor_tensor(rinv[:, 0:HB], rinv[:, 0:HB], anyv[:, HB * n:HB * n + HB], ALU.mult)\
                        .then_inc(xs_rcp, 1)
                    dve.wait_ge(xs_rcp, 2 * c + 2)
                    nc.vector.tensor_tensor(scb, scb, rinv[:, 0:HB].unsqueeze(2).broadcast_to((P, HB, P)), ALU.mult)\
                        .then_inc(xs_norm, 1)

            def add_out(c, n):
                last = isinstance(c, int) and c > 8 * (GROUPS - 1)
                if not last or n == 0:
                    dve.wait_ge(xo_mm, c)
                for b in range(HB):
                    if last and n == 1:
                        dve.wait_ge(xo_mm, c + b)
                    a = acc[:, HB * n + b, :]
                    nc.vector.tensor_tensor(a, a, OB[b][:, :], ALU.add).then_inc(xo_add, 1)
                    if last:
                        dve.wait_ge(xo_add, B * GROUPS + HB * n + b + 1)
                        stats(HB * n + b)

            def group(g):
                base = PER_GROUP * g

                def split(m, s):
                    j = SLOT[m][s]
                    pos = G0 + PER_GROUP + j
                    _, _, hi, low = group_item(j)
                    dve.wait_ge(w_ld[slot_of(pos)], 16 * (pos // RING + 1) + PER_GROUP // RING * 16 * g)
                    nc.vector.tensor_copy(hi, ring[:, slot_of(pos), :]).then_inc(w_hi, 1)
                    split_lo(pos, base, hi, low, D)

                for q in range(1, 9):
                    c = 8 * g + q
                    h = q - GROUP
                    if q == 4:
                        dve.wait_ge(xv_mm, c + 4)
                        for s in range(GROUP):
                            split("v", s)
                    quarter(c, q, True, True)
                    if 4 <= q < 8:
                        dve.wait_ge(xk_mm, c + 1)
                        split("q", h)
                        split("k", h)
                    if q % GROUP == 0:
                        if isinstance(g, int) and q == GROUP:
                            dve.wait_ge(xo_add, HB)
                        add_out(c, q // GROUP - 1)
                    if 5 <= q:
                        dve.wait_ge(xo_mm, c)
                        split("o", h - 1)
                    if isinstance(g, int) and q < len(FIRST_SPLITS):
                        group_rest(*FIRST_SPLITS[q])

            moments(1)
            group_rest(6, 8)
            quarter(0, 0, False, True)
            rms(1)
            group_rest(*FIRST_SPLITS[0])
            for b in range(HB, B):
                row_out(b)
            for b in range(HB, B):
                xtile_rest(b)
            group(0)
            with dve.Fori(1, GROUPS - 1) as g:
                group(g)

            def centre_half(n):
                moments(n, 2)
                for j in range(HB):
                    b = HB * n + j
                    if n:
                        dve.wait_ge(tp_mm, 2 * B + j + 1)
                    centre(hb[j], b).then_inc(xn_rdy, 1)

            def route(n, u):
                dve.wait_ge(low_mm, 2 * n + u + 1)
                r = slice(2 * u, 2 * u + 2)
                low = LOW[n][u][:, 0:2 * (P + E)].rearrange("p (b c) -> p b c", b=2)
                link(nc.vector.tensor_tensor(lg[:, r, :], low[:, :, P:P + E],
                                             brs[:].unsqueeze(1).broadcast_to((P, 2, E)), ALU.add))
                link(nc.vector.tensor_reduce(lmx[:, r], lg[:, r, :], AX_X, ALU.max))
                nc.vector.tensor_tensor(lg[:, r, :], lg[:, r, :], lmx[:, r].unsqueeze(2).broadcast_to((P, 2, E)),
                                        ALU.subtract).then_inc(lg_rdy, 1)
                dve.wait_ge(lg_exp, 2 * n + u + 1)
                link(nc.vector.tensor_reduce(lsum[:, r], lg[:, r, :], AX_X, ALU.add))
                link(nc.vector.reciprocal(lr[:, r], lsum[:, r]))
                link(nc.vector.tensor_scalar(lr[:, r], lr[:, r], 2.0 * E, None, ALU.mult))
                link(nc.vector.tensor_tensor(scw[:, r, :], lg[:, r, :], lr[:, r].unsqueeze(2).broadcast_to((P, 2, E)),
                                             ALU.mult))
                for j in range(2):
                    b = 2 * u + j
                    ins = nc.vector.tensor_tensor(
                        bmrow[:, n, b * P:(b + 1) * P].rearrange("p (e r) -> p e r", r=R),
                        low[:, j, 0:P].rearrange("p (e r) -> p e r", r=R),
                        scw[:, b, :].unsqueeze(2).broadcast_to((P, E, R)), ALU.mult)
                ins.then_inc(g_rdy, 1)

            def finish(b):
                dve.wait_ge(f_mm, b + 1)
                nc.vector.tensor_tensor(acc[:, b, :], acc[:, b, :], FB[b % HB][:, :], ALU.add).then_inc(f_add, 1)

            for q in range(1, 9):
                c = 8 * (GROUPS - 1) + q
                if q == 8:
                    route(0, 0)
                quarter(c, q, True, q < 8)
                if q == 8:
                    route(0, 1)
                if q % GROUP == 0:
                    add_out(c, q // GROUP - 1)
                if q == 5:
                    centre_half(0)
            centre_half(1)
            for b in range(HB):
                finish(b)
            route(1, 0)
            route(1, 1)
            for b in range(HB, B):
                finish(b)

        @block.tensor
        def _(pe):
            def three(dst, a, w, first=True, last=True):
                nc.tensor.matmul(dst, a(0), w(0), start=first, stop=False)
                nc.tensor.matmul(dst, a(1), w(0), start=False, stop=False)
                return nc.tensor.matmul(dst, a(0), w(1), start=False, stop=last)

            def tile_turn(k, src, dst):
                pe.wait_ge(xn_rdy, k + 1)
                for kt in range(KT):
                    ins = nc.tensor.transpose(dst[:, kt * P:(kt + 1) * P], src[:, kt * P:(kt + 1) * P], ident[:])
                ins.then_inc(tp_mm, 1)

            def first_turn(b):
                tile_turn(b, h1[b % HB], NB[b % HB])

            def conv(n, m, j):
                t, kt = divmod(j, KT)
                ins = three(CB[3 * n + m][:, :].rearrange("p (b t) -> p b t", b=HB),
                            lambda s: conv_r[:, s, j, m * P:(m + 1) * P],
                            lambda s: xpad_r[:, s, kt, HB * n:HB * n + HB, t:t + P],
                            j == 0, j == N_CONV - 1)
                if j == N_CONV - 1:
                    ins.then_inc(cv_mm, 1)

            pe.wait_ge(id_rdy, 2)
            for b in range(HB):
                first_turn(b)
            pe.wait_ge(xt_lo, HB)
            for m in range(3):
                for j in range(N_CONV):
                    if m == 0 and j == 0:
                        pe.wait_ge(tap0_lo, 1)
                    if m == 0 and j and j % KT == 0:
                        pe.wait_ge(tap_lo, j // KT)
                    if m == 1 and HB <= j < B:
                        first_turn(j)
                    conv(0, m, j)
            pe.wait_ge(xt_lo, B)
            for m in range(2):
                for j in range(N_CONV):
                    conv(1, m, j)

            def xvalues(dst, b):
                for kt in range(KT):
                    ins = three(dst, lambda s: ct_r[:, s, kt, b * P:(b + 1) * P],
                                lambda s: w_r["v"][:, s, kt, :], kt == 0, kt == KT - 1)
                ins.then_inc(xv_mm, 1)

            def project(b):
                three(PJ[b][:, :], lambda s: yt_r[:, s, b * P:(b + 1) * P], lambda s: proj_r[:, s, :])\
                    .then_inc(pj_mm, 1)

            def head_proj(i, m, dst, done):
                n, p_ = divmod(i, PAIRS)
                three(dst, lambda s: wqkv_r[:, s, m, p_ * P:(p_ + 1) * P],
                      lambda s: qkv_r[:, s, m, n * HALF:(n + 1) * HALF]).then_inc(done, 1)

            pe.wait_ge(cv_lo, 2)
            pe.wait_ge(w_lo, WO_AT)
            head_proj(0, 0, J0[:, :], qh_mm)
            head_proj(0, 1, J1[:, :], kh_mm)
            for j in range(N_CONV):
                conv(1, 2, j)
            pe.wait_ge(cv_lo, 5)
            for i in range(ITEMS + 2):
                if i < ITEMS:
                    pe.wait_ge(qh_sb, i + 1)
                    pe.wait_ge(kh_sb, i + 1)
                    if i:
                        pe.wait_ge(s_max, 8 * i)
                    for b in range(HB):
                        for e in range(2):
                            t, h = slice(b * P, (b + 1) * P), slice(64 * e, 64 * e + 64)
                            ins = nc.tensor.matmul(S2[e][:, t], qt[h, t], kt_[h, t], start=True, stop=True)
                    ins.then_inc(s_mm, 1)
                if 1 <= i <= ITEMS:
                    for e in range(2):
                        if i % PAIRS == 1:
                            pe.wait_ge((va_even, va_odd)[e], HB * (i // PAIRS + 1))
                        pe.wait_ge((s_even, s_odd)[e], i)
                        for b in range(HB):
                            ins = nc.tensor.transpose(T2[e][:, b * P:(b + 1) * P], sc[:, (i - 1) % 2, e, b, :], ident[:])
                    ins.then_inc(t_mm, 1)
                if i + 1 < ITEMS:
                    if i in (PROJ_I + 1, PROJ_I + 2):
                        pe.wait_ge(pj_add, 2 * (i - PROJ_I))
                    if i >= 1:
                        pe.wait_ge(va_even, HB * ((i - 1) // PAIRS + 1))
                        pe.wait_ge(va_odd, HB * ((i - 1) // PAIRS + 1))
                    head_proj(i + 1, 0, J0[:, :], qh_mm)
                    head_proj(i + 1, 1, J1[:, :], kh_mm)
                if i >= 2:
                    p_, u = (i - 2) % PAIRS, i % 2
                    pe.wait_ge(o_lo, i - 1)
                    if i == 2:
                        pe.wait_ge(w_lo, WO_AT + 2)
                    if i - 2 == PAIRS:
                        pe.wait_ge(y_lo, 1)
                    three(Y[:, :], lambda s: wo_r[:, s, p_ * P:(p_ + 1) * P], lambda s: ot_r[:, u, s, :],
                          p_ == 0, p_ == PAIRS - 1).then_inc(wo_mm, 1)
                if i == ITEMS:
                    pe.wait_ge(w_lo, G0 + GROUP)
                    xvalues(J0[:, :], 0)
                if 1 <= i <= ITEMS:
                    p_ = (i - 1) % PAIRS
                    pe.wait_ge(pt_even, i)
                    pe.wait_ge(pt_odd, i)
                    for b in range(HB):
                        for e in range(2):
                            ins = nc.tensor.matmul(PVB[64 * e:64 * e + 64, b * P:(b + 1) * P],
                                                   va[:, b, p_ * P + 64 * e:p_ * P + 64 * e + 64],
                                                   pt[:, e, b * P:(b + 1) * P], start=True, stop=True)
                    ins.then_inc(pv_mm, 1)
                if i % PAIRS == 0 and i < ITEMS:
                    n = i // PAIRS
                    for m in range(B):
                        dst = VB[n][m]
                        if dst is bank[7]:
                            pe.wait_ge(cv_lo, 6)
                        if dst in VB[n][:m]:
                            pe.wait_ge((va_even, va_odd)[m % 2], HB * n + VB[n].index(dst) // 2 + 1)
                        elif dst in (J0, J1):
                            pe.wait_ge((qh_sb, kh_sb)[m % 2], i + 2)
                        b = HB * n + m // 2
                        three(dst[:, :], lambda s: qkv_r[:, s, 2, b * P:(b + 1) * P],
                              lambda s: wqkv_r[:, s, 2, m % 2 * D:(m % 2 + 1) * D]).then_inc(va_mm, 1)
                if i == ITEMS:
                    xvalues(J1[:, :], 1)
                if i in (PROJ_I, PROJ_I + 1):
                    if i == PROJ_I:
                        pe.wait_ge(y_lo, 1)
                        pe.wait_ge(w_lo, PROJ_AT + 1)
                    for m in range(2):
                        pe.wait_ge((qh_sb, kh_sb)[m], i + 2)
                        project(2 * (i - PROJ_I) + m)
            def second_turn(b):
                tile_turn(B + b, hb[b % HB], XB[b])

            pe.wait_ge(xv_sb, 1)
            xvalues(J0[:, :], 2)
            second_turn(0)
            second_turn(1)
            pe.wait_ge(y_lo, 2)
            for b in range(HB, B):
                project(b)
            for b in (2, 3):
                pe.wait_ge(xt_lo, B + b - 1)
                second_turn(b)
            pe.wait_ge(xv_sb, 2)
            xvalues(J1[:, :], 3)

            def xproj(dst, m, h, n):
                src = xt_r if m == "q" else ct_r
                for kt in range(KT):
                    ins = three(dst, lambda s: w_r[m][:, s, h, kt * P:(kt + 1) * P],
                                lambda s: src[:, s, kt, n * HALF:(n + 1) * HALF], kt == 0, kt == KT - 1)
                return ins

            def quarter(g, q, back, front):
                c = 8 * g + q
                h, n = q % GROUP, q // GROUP % 2
                hp, np_ = (q - 1) % GROUP, (q - 1) // GROUP % 2
                at = PER_GROUP * g + G0 + PER_GROUP * (q // 8)
                if front:
                    if n == 0:
                        pe.wait_ge(w_lo, at + SLOT["q"][h] + 1)
                    if front != "last" or q == GROUP:
                        pe.wait_ge(xv_sb, c + 4)
                    if front == "last" and q == 7:
                        pe.wait_ge(xt_hi, 2 * B + 2)
                    xproj(J0[:, :], "q", h, n).then_inc(xq_mm, 1)
                if back:
                    pe.wait_ge(xs_norm, c)
                    for b in range(HB):
                        ins = nc.tensor.transpose(TX[:, b * P:(b + 1) * P], scb[:, b, :], ident[:])
                    ins.then_inc(xt_mm, 1)
                if front:
                    if n == 0:
                        pe.wait_ge(w_lo, at + SLOT["k"][h] + 1)
                    xproj(J1[:, :], "k", h, n).then_inc(xk_mm, 1)
                if isinstance(c, int) and c == 1:
                    for b in range(HB, B):
                        second_turn(b)
                if back and not front:
                    low_rank(0, 0)
                if back:
                    pe.wait_ge(xp_sb, c)
                    for b in range(HB):
                        t = slice(b * P, (b + 1) * P)
                        ins = nc.tensor.matmul(TX[:, t], vals[:, np_, b, hp * P:(hp + 1) * P], pt[:, 0, t],
                                               start=True, stop=True)
                    ins.then_inc(xpv_mm, 1)
                if front:
                    pe.wait_ge(xq_sb, c + 1)
                    pe.wait_ge(xk_sb, c + 1)
                    if isinstance(c, int) and c == 0:
                        pe.wait_ge(pj_add, B)
                    for b in range(HB):
                        t = slice(b * P, (b + 1) * P)
                        ins = nc.tensor.matmul(SX[:, t], qt[:, t], kt_[:, t], start=True, stop=True)
                    ins.then_inc(xs_mm, 1)
                    if front != "last":
                        if q == GROUP:
                            pe.wait_ge(w_lo, at + PER_GROUP + GROUP)
                        xvalues(J0[:, :], HB * (1 - n) + h)
                    elif q in (6, 7):
                        adapter_turn(2 * q - 12)
                        adapter_turn(2 * q - 11)
                if back and not front:
                    low_rank(0, 1)
                if back:
                    if q <= GROUP:
                        pe.wait_ge(w_lo, at + SLOT["o"][hp] + 1)
                    if hp == 0 and not (isinstance(c, int) and c == 1):
                        pe.wait_ge(xo_add, B * g + B + HB * (q // GROUP))
                    if isinstance(c, int) and c == 1:
                        pe.wait_ge(xt_lo, 2 * B)
                    pe.wait_ge(xo_lo, c)
                    for b in range(HB):
                        ins = three(OB[b][:, :], lambda s: r_o[:, s, b * P:(b + 1) * P],
                                    lambda s: w_r["o"][:, s, hp, :], hp == 0, hp == GROUP - 1)
                        if b == HB - 1 or not front:
                            ins.then_inc(xo_mm, 1)

            pe.wait_ge(xt_lo, B + HB)
            quarter(0, 0, False, True)
            for q in range(1, 9):
                quarter(0, q, True, True)
            with pe.Fori(1, GROUPS - 1) as g:
                for q in range(1, 9):
                    quarter(g, q, True, True)

            def adapter_turn(b):
                tile_turn(2 * B + b, hb[b % HB], TURN[b])

            def low_rank(n, u):
                pe.wait_ge(xt_hi, 2 * B + (HB + 2 * u + 2 if n else HB))
                for j in (2 * u, 2 * u + 1):
                    for kt in range(KT):
                        ins = nc.tensor.matmul(LOW[n][u][:, j % 2 * (P + E):(j % 2 + 1) * (P + E)],
                                               vals[:, 0, j, kt * P:(kt + 1) * P], aws[:, kt, :],
                                               start=kt == 0, stop=kt == KT - 1)
                ins.then_inc(low_mm, 1)

            def combine(n):
                def turn(u):
                    pe.wait_ge(g_rdy, 2 * n + u + 1)
                    for j in (2 * u, 2 * u + 1):
                        ins = nc.tensor.transpose(GT[n][u][:, j % 2 * P:(j % 2 + 1) * P],
                                                  bmrow[:, n, j * P:(j + 1) * P], ident[:])
                    ins.then_inc(gt_mm, 1)

                def outputs(u):
                    pe.wait_ge(gt_sb, 2 * n + u + 1)
                    for j in (2 * u, 2 * u + 1):
                        if n:
                            pe.wait_ge(f_add, j + 1)
                        nc.tensor.matmul(FB[j][:, :], kt_[:, j * P:(j + 1) * P], bws[:], start=True, stop=True)\
                            .then_inc(f_mm, 1)

                turn(0)
                if n == 0:
                    turn(1)
                outputs(0)
                if n:
                    turn(1)
                outputs(1)

            for q in range(1, 9):
                quarter(GROUPS - 1, q, True, False if q == 8 else "last" if q >= GROUP else True)
            combine(0)
            for b in range(HB, B):
                if b >= HB + 2:
                    pe.wait_ge(xt_hi, 2 * B + b - 1)
                adapter_turn(b)
            low_rank(1, 0)
            low_rank(1, 1)
            combine(1)


N_CST = 9


def kernel(**inputs):
    import numpy as _np
    import concourse.bacc as _bacc
    from concourse import mybir as _mybir
    from concourse.bass_utils import run_bass_kernel_spmd as _run

    a = {k.replace("L0_", ""): _np.asarray(v) for k, v in inputs.items()}

    def heads(w):
        return w.reshape(XH, P, KT, P).transpose(0, 3, 2, 1).reshape(XH, P, D)

    xv = a["xattn_w_v"].reshape(GROUPS, D, KT, P).transpose(0, 2, 3, 1).reshape(XH, P, D)
    layout = {
        "x": a["x"],
        "ctx_t": a["ctx_4096"].reshape(TOK, D).T,
        "mask": a["mask_BxSxS2_bk0"],
        "conv_w": a["attn_conv_w"],
        "conv_b": a["attn_conv_b"].reshape(3, P).T,
        "wq": a["attn_wq"].reshape(P, 2 * D), "wk": a["attn_wk"].reshape(P, 2 * D), "wv": a["attn_wv"].reshape(P, 2 * D),
        "bq": a["attn_bq"].reshape(PAIRS, P).T, "bk": a["attn_bk"].reshape(PAIRS, P).T,
        "bv": a["attn_bv"].reshape(PAIRS, P).T,
        "wo": a["attn_wo"].reshape(2 * D, P),
        "bo": a["attn_bo"].reshape(P, 1),
        "proj_w": a["attn_proj_w"],
        "proj_b": a["attn_proj_b"],
        "pos": a["xattn_position_bias"],
        "lnw": a["xattn_ln_weight"],
        "xq": heads(a["xattn_w_q"]), "xk": heads(a["xattn_w_k"]), "xv": xv,
        "xo": a["xattn_w_out"].T.reshape(XH, P, D),
        "aw": _np.concatenate([a["ffn_A"].reshape(E * R, D).T, a["ffn_Wr"].T], axis=1),
        "bw": a["ffn_B"].transpose(0, 2, 1).reshape(E * R, D),
        "br": a["ffn_br"],
    }
    nc = _bacc.Bacc("TRN2", target_bir_lowering=False, num_devices=1)
    arrays, args = {}, []
    for name, v in layout.items():
        v = _np.ascontiguousarray(v)
        arrays[f"in_{name}"] = v
        args.append(nc.dram_tensor(f"in_{name}", v.shape, _mybir.dt.from_np(v.dtype), kind="ExternalInput").ap())
    args.append(nc.dram_tensor("out_x", (B, P, D), _mybir.dt.float32, kind="ExternalOutput").ap())
    decoder_layer(nc, *args)
    r = _run(nc, [arrays], core_ids=[0])
    return r.results[0]["out_x"]
```
